# Optimizing a Trainium2 kernel written in Bass

```python
import numpy as np
import jax
import jax.numpy as jnp

def _softmax(x, axis=-1):
    return jax.nn.softmax(x, axis=axis)

def _gelu(x):
    return jax.nn.gelu(x, approximate=True)

def _silu(x):
    return jax.nn.silu(x)

def _sigmoid(x):
    return jax.nn.sigmoid(x)

def _layernorm(x, axis=-1, eps=1e-05):
    m = jnp.mean(x, axis=axis, keepdims=True)
    v = jnp.var(x, axis=axis, keepdims=True)
    return (x - m) / jnp.sqrt(v + eps)

def _scatter_add(tgt, idx, src, axis=0):
    return tgt.at[idx].add(src)

def _segment_sum(src, seg, n):
    return jax.ops.segment_sum(src, seg, n)
kernel_name = 'mk_seq_preln_d1_jaxref_r8_ae5e54'

def setup_inputs(seed: int=0):
    np.random.seed(seed)
    _w = jnp.asarray

    def _L0_attn_setup():
        import jax, jax.numpy as jnp
        import numpy as np
        NUM_HEAD = 16
        D_Q = 64
        D_KV = 64
        ROPE_BASE = 10000.0

        def _cos_sin(seq_len, dim):
            pos = jnp.arange(seq_len, dtype=jnp.float32)[:, None]
            ids = jnp.arange(dim // 2, dtype=jnp.float32)
            theta = ROPE_BASE ** (-2.0 * ids) / (dim // 2)
            r = pos * theta[None, :]
            return (jnp.cos(r), jnp.sin(r))

        def _rope(x, cos, sin):
            b, s, d = x.shape
            xv = x.reshape(b, s, d // 2, 2)
            x0, x1 = (xv[..., 0], xv[..., 1])
            out = jnp.stack([x0 * cos - x1 * sin, x1 * cos + x0 * sin], axis=-1)
            return out.reshape(b, s, d)
        key = jax.random.key(seed)
        ks = jax.random.split(key, 10)
        d_model, d_q, d_kv = (128, D_Q, D_KV)
        b, s = (2, 256)
        w = lambda k, i, o: jax.random.normal(k, (i, o), dtype=jnp.float32) * 0.02
        return {'x': jax.random.normal(ks[0], (b, s, d_model), dtype=jnp.float32), 'Wd_q_w': w(ks[1], d_model, d_q), 'Wd_q_b': jnp.zeros((d_q,), jnp.float32), 'Wu_q_w': w(ks[2], d_q, d_model), 'Wu_q_b': jnp.zeros((d_model,), jnp.float32), 'Wq_r_w': w(ks[3], d_q, d_model), 'Wq_r_b': jnp.zeros((d_model,), jnp.float32), 'Wk_r_w': w(ks[4], d_model, d_model), 'Wk_r_b': jnp.zeros((d_model,), jnp.float32), 'Wd_kv_w': w(ks[5], d_model, d_kv), 'Wd_kv_b': jnp.zeros((d_kv,), jnp.float32), 'Wu_k_w': w(ks[6], d_kv, d_model), 'Wu_k_b': jnp.zeros((d_model,), jnp.float32), 'Wu_v_w': w(ks[7], d_kv, d_model), 'Wu_v_b': jnp.zeros((d_model,), jnp.float32), 'Wo_w': w(ks[8], d_model, d_model), 'Wo_b': jnp.zeros((d_model,), jnp.float32)}
    _L0_attn_in = _L0_attn_setup()

    def _L0_ffn_setup():
        import jax, jax.numpy as jnp
        import numpy as np
        B, L, D = (1, 256, 128)
        E, H, G, K = (64, 32, 64, 16)

        def _grouped_routing_scores(router_scores):
            T, En = router_scores.shape
            Tq = T // G
            budget = Tq * K
            order = jnp.argsort(-router_scores, axis=0)
            sorted_vals = jnp.take_along_axis(router_scores, order, axis=0)
            group_score = sorted_vals.reshape(Tq, G, En).sum(axis=1)
            _, top_flat = jax.lax.top_k(group_score.reshape(-1), budget)
            gmask = jnp.zeros((Tq * En,), bool).at[top_flat].set(True).reshape(Tq, En)
            mask_sorted = jnp.broadcast_to(gmask[:, None, :], (Tq, G, En)).reshape(T, En)
            mask = jnp.zeros((T, En), bool).at[order, jnp.arange(En)[None, :]].set(mask_sorted)
            fs = jnp.where(mask, router_scores, 0.0)
            return fs / (fs.sum(axis=-1, keepdims=True) + 1e-06)
        key = jax.random.key(seed)
        ks = jax.random.split(key, 6)
        s = lambda k, shape, scale: jax.random.normal(k, shape, jnp.float32) * scale
        return {'x': jax.random.normal(ks[0], (B, L, D), jnp.float32), 'Wr': s(ks[1], (D, E), D ** (-0.5)), 'br': jnp.zeros((E,), jnp.float32), 'Wup': s(ks[2], (E, D, H), D ** (-0.5)), 'bup': jnp.zeros((E, H), jnp.float32), 'Wgate': s(ks[3], (E, D, H), D ** (-0.5)), 'bgate': jnp.zeros((E, H), jnp.float32), 'Wdown': s(ks[4], (E, H, D), H ** (-0.5)), 'bdown': jnp.zeros((E, D), jnp.float32)}
    _L0_ffn_in = _L0_ffn_setup()
    _d = {'L0_attn_x': _L0_attn_in['x'], 'L0_attn_Wd_q_w': _L0_attn_in['Wd_q_w'], 'L0_attn_Wd_q_b': _L0_attn_in['Wd_q_b'], 'L0_attn_Wu_q_w': _L0_attn_in['Wu_q_w'], 'L0_attn_Wu_q_b': _L0_attn_in['Wu_q_b'], 'L0_attn_Wq_r_w': _L0_attn_in['Wq_r_w'], 'L0_attn_Wq_r_b': _L0_attn_in['Wq_r_b'], 'L0_attn_Wk_r_w': _L0_attn_in['Wk_r_w'], 'L0_attn_Wk_r_b': _L0_attn_in['Wk_r_b'], 'L0_attn_Wd_kv_w': _L0_attn_in['Wd_kv_w'], 'L0_attn_Wd_kv_b': _L0_attn_in['Wd_kv_b'], 'L0_attn_Wu_k_w': _L0_attn_in['Wu_k_w'], 'L0_attn_Wu_k_b': _L0_attn_in['Wu_k_b'], 'L0_attn_Wu_v_w': _L0_attn_in['Wu_v_w'], 'L0_attn_Wu_v_b': _L0_attn_in['Wu_v_b'], 'L0_attn_Wo_w': _L0_attn_in['Wo_w'], 'L0_attn_Wo_b': _L0_attn_in['Wo_b'], 'L0_ffn_Wr': _L0_ffn_in['Wr'], 'L0_ffn_br': _L0_ffn_in['br'], 'L0_ffn_Wup': _L0_ffn_in['Wup'], 'L0_ffn_bup': _L0_ffn_in['bup'], 'L0_ffn_Wgate': _L0_ffn_in['Wgate'], 'L0_ffn_bgate': _L0_ffn_in['bgate'], 'L0_ffn_Wdown': _L0_ffn_in['Wdown'], 'L0_ffn_bdown': _L0_ffn_in['bdown']}
    _x0 = _d['L0_attn_x']
    _d['L0_attn_x'] = jax.random.normal(jax.random.fold_in(jax.random.key(seed), 1), (4, 512, 128), dtype=_x0.dtype)
    del _x0
    return _d

def reference(L0_attn_x, L0_attn_Wd_q_w, L0_attn_Wd_q_b, L0_attn_Wu_q_w, L0_attn_Wu_q_b, L0_attn_Wq_r_w, L0_attn_Wq_r_b, L0_attn_Wk_r_w, L0_attn_Wk_r_b, L0_attn_Wd_kv_w, L0_attn_Wd_kv_b, L0_attn_Wu_k_w, L0_attn_Wu_k_b, L0_attn_Wu_v_w, L0_attn_Wu_v_b, L0_attn_Wo_w, L0_attn_Wo_b, L0_ffn_Wr, L0_ffn_br, L0_ffn_Wup, L0_ffn_bup, L0_ffn_Wgate, L0_ffn_bgate, L0_ffn_Wdown, L0_ffn_bdown):

    def _L0_attn_ref(x, Wd_q_w, Wd_q_b, Wu_q_w, Wu_q_b, Wq_r_w, Wq_r_b, Wk_r_w, Wk_r_b, Wd_kv_w, Wd_kv_b, Wu_k_w, Wu_k_b, Wu_v_w, Wu_v_b, Wo_w, Wo_b):
        import jax, jax.numpy as jnp
        import numpy as np
        NUM_HEAD = 16
        D_Q = 64
        D_KV = 64
        ROPE_BASE = 10000.0

        def _cos_sin(seq_len, dim):
            pos = jnp.arange(seq_len, dtype=jnp.float32)[:, None]
            ids = jnp.arange(dim // 2, dtype=jnp.float32)
            theta = ROPE_BASE ** (-2.0 * ids) / (dim // 2)
            r = pos * theta[None, :]
            return (jnp.cos(r), jnp.sin(r))

        def _rope(x, cos, sin):
            b, s, d = x.shape
            xv = x.reshape(b, s, d // 2, 2)
            x0, x1 = (xv[..., 0], xv[..., 1])
            out = jnp.stack([x0 * cos - x1 * sin, x1 * cos + x0 * sin], axis=-1)
            return out.reshape(b, s, d)
        b, s, d_model = x.shape
        h = NUM_HEAD
        hd = d_model // h
        scale = jnp.sqrt(jnp.float32(h + D_KV + D_Q))

        def heads(t):
            return t.reshape(b, s, h, hd).transpose(0, 2, 1, 3)
        cos, sin = _cos_sin(s, d_model)
        ct_q = x @ Wd_q_w + Wd_q_b
        qt_c = heads(ct_q @ Wu_q_w + Wu_q_b)
        qt_r = heads(_rope(ct_q @ Wq_r_w + Wq_r_b, cos, sin))
        query = qt_c + qt_r
        ct_kv = x @ Wd_kv_w + Wd_kv_b
        kt_c = heads(ct_kv @ Wu_k_w + Wu_k_b)
        kt_r = heads(_rope(x @ Wk_r_w + Wk_r_b, cos, sin))
        key = kt_c + kt_r
        value = heads(ct_kv @ Wu_v_w + Wu_v_b)
        attn = jnp.einsum('bhqd,bhkd->bhqk', query, key) / scale
        attn = jax.nn.softmax(attn, axis=-1)
        out = jnp.einsum('bhqk,bhkd->bhqd', attn, value)
        out = out.transpose(0, 2, 1, 3).reshape(b, s, d_model)
        return out @ Wo_w + Wo_b

    def _L0_ffn_ref(x, Wr, br, Wup, bup, Wgate, bgate, Wdown, bdown):
        import jax, jax.numpy as jnp
        import numpy as np
        B, L, D = (1, 256, 128)
        E, H, G, K = (64, 32, 64, 16)

        def _grouped_routing_scores(router_scores):
            T, En = router_scores.shape
            Tq = T // G
            budget = Tq * K
            order = jnp.argsort(-router_scores, axis=0)
            sorted_vals = jnp.take_along_axis(router_scores, order, axis=0)
            group_score = sorted_vals.reshape(Tq, G, En).sum(axis=1)
            _, top_flat = jax.lax.top_k(group_score.reshape(-1), budget)
            gmask = jnp.zeros((Tq * En,), bool).at[top_flat].set(True).reshape(Tq, En)
            mask_sorted = jnp.broadcast_to(gmask[:, None, :], (Tq, G, En)).reshape(T, En)
            mask = jnp.zeros((T, En), bool).at[order, jnp.arange(En)[None, :]].set(mask_sorted)
            fs = jnp.where(mask, router_scores, 0.0)
            return fs / (fs.sum(axis=-1, keepdims=True) + 1e-06)
        Bx, Lx, Dx = x.shape
        xt = x.reshape(-1, Dx)
        router_scores = jax.nn.softmax(xt @ Wr + br, axis=-1)
        fs = _grouped_routing_scores(router_scores)
        up = jnp.einsum('td,edh->teh', xt, Wup) + bup
        gate = jnp.einsum('td,edh->teh', xt, Wgate) + bgate
        h = jax.nn.silu(up) * gate * fs[:, :, None]
        out = jnp.einsum('teh,ehd->td', h, Wdown) + fs @ bdown
        return out.reshape(Bx, Lx, Dx)
    x = L0_attn_x
    x = x + _L0_attn_ref(_layernorm(x, axis=-1), L0_attn_Wd_q_w, L0_attn_Wd_q_b, L0_attn_Wu_q_w, L0_attn_Wu_q_b, L0_attn_Wq_r_w, L0_attn_Wq_r_b, L0_attn_Wk_r_w, L0_attn_Wk_r_b, L0_attn_Wd_kv_w, L0_attn_Wd_kv_b, L0_attn_Wu_k_w, L0_attn_Wu_k_b, L0_attn_Wu_v_w, L0_attn_Wu_v_b, L0_attn_Wo_w, L0_attn_Wo_b)
    x = x + _L0_ffn_ref(_layernorm(x, axis=-1), L0_ffn_Wr, L0_ffn_br, L0_ffn_Wup, L0_ffn_bup, L0_ffn_Wgate, L0_ffn_bgate, L0_ffn_Wdown, L0_ffn_bdown)
    return x

_drawn_inputs = setup_inputs


def setup_inputs(seed=0):
    import zlib

    import numpy as np

    out = dict(_drawn_inputs(seed))
    spreads = {'L0_attn_Wd_q_b': (0.0, 0.8),
     'L0_attn_Wu_q_b': (0.0, 0.8),
     'L0_attn_Wq_r_b': (0.0, 0.8),
     'L0_attn_Wk_r_b': (0.0, 0.8),
     'L0_attn_Wd_kv_b': (0.0, 0.8),
     'L0_attn_Wu_k_b': (0.0, 0.8),
     'L0_attn_Wu_v_b': (0.0, 0.305),
     'L0_attn_Wo_b': (0.0, 0.1),
     'L0_ffn_br': (0.0, 0.1),
     'L0_ffn_bup': (0.0, 0.444),
     'L0_ffn_bgate': (0.0, 0.457),
     'L0_ffn_bdown': (0.0, 0.27)}
    factors = {'L0_attn_Wd_q_w': 8.0,
     'L0_attn_Wu_q_w': 8.0,
     'L0_attn_Wq_r_w': 8.0,
     'L0_attn_Wk_r_w': 8.0,
     'L0_attn_Wd_kv_w': 8.0,
     'L0_attn_Wu_k_w': 8.0,
     'L0_attn_Wu_v_w': 8.0}
    for name, (base, spread) in spreads.items():
        noise = np.random.default_rng([zlib.crc32(name.encode()), seed]).standard_normal(out[name].shape)
        drawn = base * np.exp(spread * noise) if base else spread * noise
        out[name] = jnp.asarray(drawn.astype(out[name].dtype))
    for name, factor in factors.items():
        out[name] = (out[name] * factor).astype(out[name].dtype)
    return out
```

```python
from contextlib import ExitStack

import concourse.bass as bass
from concourse import mybir

F32 = mybir.dt.float32
BF16 = mybir.dt.bfloat16
I32 = mybir.dt.int32
ALU = mybir.AluOpType
ACT = mybir.ActivationFunctionType
AX = mybir.AxisListType.X

P = 128
B, S, D = 4, 512, 128
NT = S // P
H, HD = 16, 8
LAT = 64
E, HE = 64, 32
GRP, TOPK = 64, 16
TOK = B * S
BUDGET = TOK // GRP * TOPK
HALF = TOK // 2
NB = HALF // GRP
RUN = S // 2
NE = E * HE // P
EPT = P // HE
SCALE = 1.0 / float(H + LAT + LAT) ** 0.5
EPS = 1e-5
QROWS = 48
MROWS = 2
KST = QROWS + MROWS
NPRE, NPOST = 9, 7
NQ = 4
UQ = 2 * NT
NQUAD = B * NQ
ST_LAG = 28
PV_LAG = 5
PT = 8
SORT = [(m, d) for m in (2 ** k for k in range(1, 11)) for d in [0] + [m >> j for j in range(2, 11) if m >> j]]
STAGES_RUN = sum(m <= 256 for m, _ in SORT)
STAGES_PAIR = sum(m <= 512 for m, _ in SORT)
SLOTS = 16 * NQUAD + ST_LAG + 2 * PV_LAG + 2
DIGITS = 8

WD, WKR, WKRS, WR, WO = 0, 128, 256, 384, 448
WUQ, WQR, WQRS = 0, 128, 256
WUK, WUV = 0, 128
CBD, CCQ, CAQ, CBQ, CCK, CAK, CBK, CUP, CGT = 0, 1, 2, 3, 4, 5, 6, 7, 23
KID, KCOS, KSIN = 0, 128, 640
KTRI, KBLK, KH01, KPAIR, KOTHER, KNEXT, KONE = 0, 128, 256, 384, 512, 640, 768
KEND = 896


def pre_base(b):
    return b * NPRE + max(b - 2, 0) * NPOST


def post_base(b):
    return min(b + 3, B) * NPRE + b * NPOST


def pre_slot(b, k):
    return 64 * (b - 1) + 8 + 3 * k if b else k - NPRE


POST_AT = [34, 37, 40, 43, 51, 54, 61]


def post_slot(b, k):
    return 64 * (b + 1) + POST_AT[k]


def nat_use(n):
    return n + max(0, (n + 12) // 16 - 1)


def mt_use(g):
    return min(16 * (g + 1) + 4, 16 * NQUAD) + g


def build(nc, x, wa, wb, cols, rows, wup, wgate, wdown, bdown, trig, cst, selc, kdig, out):
    ctx = ExitStack()
    with ctx:
        def sb(name, shape, dt=F32):
            return ctx.enter_context(nc.sbuf_tensor(name, shape, dt))

        def sem(name):
            return ctx.enter_context(nc.semaphore(name))

        parts_dram = nc.dram_tensor("parts_dram", (B, 2, 2, 3 * 8, 8 * S), BF16, kind="Internal").ap()

        wa_s = sb("wa_s", [P, 576])
        wb_s = sb("wb_s", [P, 384])
        cols_s = sb("cols_s", [P, 39])
        rows_s = sb("rows_s", [P, 320])
        wup_s = sb("wup_s", [P, NE * P])
        wgate_s = sb("wgate_s", [P, NE * P])
        wdown_s = sb("wdown_s", [P, NE, P])
        bdown_s = sb("bdown_s", [E, P])
        cst_s = sb("cst_s", [P, KEND])
        selc_s = sb("selc_s", [96, 8 * P])
        sel_s = sb("sel_s", [96, 8 * P], BF16)
        kdig_s = sb("kdig_s", [P, DIGITS, 16], I32)
        trig_s = sb("trig_s", [P, 1152])
        ident = trig_s[:, KID:KID + P]
        identb = sb("identb", [P, P], BF16)
        cosT, sinT = trig_s[:, KCOS:KCOS + S], trig_s[:, KSIN:KSIN + S]
        xin = sb("xin", [P, B, NT, P])
        xbo = sb("xbo", [P, NT, P])
        stats = sb("stats", [P, NT, 6])
        mv = sb("mv", [P, NT, 2])
        rstd = sb("rstd", [P, NT])
        vare = sb("vare", [P, NT])
        half_neg = sb("half_neg", [P, NT])
        xn = sb("xn", [P, NT, P])
        xnT = sb("xnT", [P, S])
        ctT = sb("ctT", [P, S])
        rope = sb("rope", [P, 2, 3, S])
        parts = sb("parts", [P, 2, 3, S], BF16)
        qst = sb("qst", [P, 2, 8, S], BF16)
        kst = sb("kst", [P, 2, 8, S], BF16)
        vaug = sb("vaug", [P, 2, NT, H, 32])
        mx = sb("mx", [P, 2, NT, 4])
        mpart = sb("mpart", [P, 2, NT, MROWS, 4], BF16)
        mts = sb("mts", [4 * MROWS, 2, S], BF16)
        pt = sb("pt", [P, PT, 2, S])
        osb = sb("osb", [P, 2, S])
        rden = sb("rden", [P, 2, NT * 8])
        ot = sb("ot", [P, NT, P])
        otT = sb("otT", [P, NT, P])
        x2 = sb("x2", [P, B, NT, P])
        x2T = sb("x2T", [P, TOK])
        sc = sb("sc", [P, NT, E])
        srow = sb("srow", [P, 3, NT])
        scT = sb("scT", [P, HALF])
        ping = [sb("ping0", [P, HALF]), sb("ping1", [P, HALF])]
        pt_f = pt[:, :, :, :].rearrange("p a b t -> p (a b t)")
        other = pt_f[:, 0:HALF]
        kst_f = kst[:, :, :, :].rearrange("p a h t -> p (a h t)")
        fsp = kst_f[:, 0:3 * HALF].rearrange("p (c t) -> p c t", c=3)
        msf = kst_f[0:E, 3 * HALF:3 * HALF + 2 * TOK].bitcast(F32)
        fs = qst[0:96, :, :, :].rearrange("p a h t -> p (a h t)")[:, 0:2 * TOK].rearrange("p (a t) -> p a t", a=2)
        gsum = sb("gsum", [P, NB])
        gmin = sb("gmin", [P, NB])
        cand = sb("cand", [P, 16], I32)
        ge = sb("ge", [P, 16, NB])
        cnt = sb("cnt", [P, 16])
        prefix = sb("prefix", [P, 1], I32)
        pick = sb("pick", [P, 16])
        gt = sb("gt", [P, NB])
        eq = sb("eq", [P, NB])
        gr = sb("gr", [P, 6, NB])
        one = sb("one", [P, 16])
        rt = sb("rt", [P, 40])
        eqc = sb("eqc", [P, B])
        eqo = sb("eqo", [P, 2, B])
        trow = sb("trow", [1, 2 * P])
        rtok = sb("rtok", [P, B * NT])
        vaug_f = vaug[:, :, :, :, :].rearrange("p a k h c -> p (a k h c)").rearrange("p (n t) -> p n t", t=S)
        act_s, u_s, h_s, yT = vaug_f[:, 0:2], vaug_f[:, 2:4], vaug_f[:, 4:7], vaug_f[:, 7]
        y_s = sb("y_s", [P, 2, NT, P])

        bank = [ctx.enter_context(nc.psum_tensor(f"bank{i}", [P, 512], F32)) for i in range(2)]
        stp = ctx.enter_context(nc.psum_tensor("stp", [P, 2, 2, S], F32))
        obank = ctx.enter_context(nc.psum_tensor("obank", [P, S], F32))
        misc = ctx.enter_context(nc.psum_tensor("misc", [P, 512], F32))

        loaded_w = sem("loaded_w")
        loaded_x = [sem(f"loaded_x{b}") for b in range(B)]
        loaded_ffn = sem("loaded_ffn")
        consts_ready = sem("consts_ready")
        vzero = sem("vzero")
        misc_filled = sem("misc_filled")
        misc_free = sem("misc_free")
        xn_ready = sem("xn_ready")
        var_ready = sem("var_ready")
        rstd_ready = sem("rstd_ready")
        parts_ready = sem("parts_ready")
        parts_stored = [sem(f"parts_stored{b}") for b in range(B)]
        stacks_ready = [sem(f"stacks_ready{i}") for i in range(2)]
        nat_filled = sem("nat_filled")
        nat_free = sem("nat_free")
        mparts_ready = sem("mparts_ready")
        mrows_ready = [sem(f"mrows_ready{i}") for i in range(2)]
        st_filled = sem("st_filled")
        exp_done = sem("exp_done")
        pv_done = sem("pv_done")
        o_out = sem("o_out")
        xbo_ready = sem("xbo_ready")
        xn2_ready = sem("xn2_ready")
        logits_ready = sem("logits_ready")
        rexp_ready = sem("rexp_ready")
        sc_ready = sem("sc_ready")
        swap_in = sem("swap_in")
        swapped = sem("swapped")
        rmat_in = sem("rmat_in")
        rmat_out = sem("rmat_out")
        fsp_ready = sem("fsp_ready")
        fs_ready = sem("fs_ready")
        den_done = sem("den_done")
        up_filled = sem("up_filled")
        gate_filled = sem("gate_filled")
        mask_filled = sem("mask_filled")
        silu_done = sem("silu_done")
        u_done = sem("u_done")
        h_done = sem("h_done")
        down_done = sem("down_done")
        yT_ready = sem("yT_ready")
        yt_filled = sem("yt_filled")
        y_ready = sem("y_ready")
        stored = [sem("stored0"), sem("stored1")]
        dve_step = sem("dve_step")
        pool_step = sem("pool_step")

        block = ctx.enter_context(nc.Block())

        def h2(q, g1):
            return 4 * (q // 2) + 2 * g1 + q % 2

        @block.sync
        def _(sp):
            sp.dma_start(xin[:, 0], x[0].rearrange("(p i) d -> p i d", i=NT)).then_inc(loaded_x[0], 16)
            for dst, src in ((trig_s[:, KCOS:], trig[:, KCOS:]), (rows_s[:, :], rows[0].partition_broadcast(P))):
                sp.dma_start(dst, src).then_inc(loaded_w, 16)
            for b in range(1, B):
                sp.dma_start(xin[:, b], x[b].rearrange("(p i) d -> p i d", i=NT)).then_inc(loaded_x[b], 16)
            for dst, src in ((wup_s[:, :], wup), (wgate_s[:, :], wgate),
                             (wdown_s[:, :, :], wdown.rearrange("p (n d) -> p n d", n=NE)),
                             (bdown_s[:, :], bdown), (selc_s[:, :], selc), (cst_s[:, :], cst),
                             (kdig_s[:, :, :], kdig.rearrange("p (s k) -> p s k", k=16))):
                sp.dma_start(dst, src).then_inc(loaded_ffn, 16)

            def stack(b):
                for a in range(2):
                    sp.wait_ge(parts_ready, 2 * b + a + 1)
                    for hp in range(2):
                        sp.dma_start(parts_dram[b, a, hp].rearrange("(c d) (h t) -> (d h) c t", c=3, h=8),
                                     parts[64 * hp:64 * hp + 64, a]).then_inc(parts_stored[b], 16)
                sp.wait_ge(parts_stored[b], 64)
                if b >= 2:
                    sp.wait_ge(st_filled, 32 * (b - 1))
                for hp in range(2):
                    for r0, reps in ((0, 3), (24, 2), (40, 1)):
                        src = parts_dram[b, 0, hp, 0:8 * reps]
                        r = 64 * hp + r0
                        sp.dma_start(qst[r:r + 8 * reps, b % 2], src.rearrange("r (h t) -> r h t", h=8))\
                          .then_inc(stacks_ready[b % 2], 16)
                    for c in range(6):
                        part = (0, 0, 0, 1, 1, 2)[c]
                        src = parts_dram[b, 1, hp, 8 * part:8 * part + 8]
                        r = 64 * hp + 8 * c
                        sp.dma_start(kst[r:r + 8, b % 2], src.rearrange("r (h t) -> r h t", h=8))\
                          .then_inc(stacks_ready[b % 2], 16)

            def mrows(g):
                b, q = divmod(g, NQ)
                sp.wait_ge(nat_free, mt_use(g) + 1)
                for p in range(MROWS):
                    for hp in range(2):
                        a = h2(q, 0)
                        r, m = 64 * hp + QROWS + p, 4 * p + 2 * hp
                        sp.dma_start(qst[r:r + 1, b % 2, a:a + 3:2, :], mts[m:m + 2, g % 2, :])\
                          .then_inc(mrows_ready[g % 2], 16)

            stack(0)
            for b in range(B):
                for q in range(NQ):
                    if q == 2 and b + 1 < B:
                        stack(b + 1)
                    mrows(NQ * b + q)
            sp.wait_ge(swap_in, 1)
            for k in range(2):
                sp.dma_start(other[64 * k:64 * k + 64, :], ping[0][64 - 64 * k:128 - 64 * k, :]).then_inc(swapped, 16)
            sp.wait_ge(fsp_ready, 3)
            for half in range(2):
                tok = msf.rearrange("e (b h t) -> e b h t", b=B, h=2)[:, :, half]
                sp.dma_start(tok, ping[0][64 * half:64 * half + 64, :].rearrange("e (b t) -> e b t", b=B))\
                  .then_inc(fs_ready, 16)
                for part in range(3):
                    for eg in range(2):
                        r = 64 * half + 32 * eg
                        tok = fs[32 * part:32 * part + 32, eg].rearrange("e (b h t) -> e b h t", b=B, h=2)[:, :, half]
                        sp.dma_start(tok, fsp[r:r + 32, part].rearrange("e (b t) -> e b t", b=B)).then_inc(fs_ready, 16)
            for blk in range(B):
                sp.wait_ge(y_ready, blk + 1)
                sp.dma_start(out[blk].rearrange("(p i) d -> p i d", i=NT), y_s[:, blk % 2])\
                  .then_inc(stored[blk % 2], 16)
            for k in range(2):
                sp.wait_ge(stored[k], 16 * B // 2)

        @block.gpsimd
        def _(pool):
            steps = [0]

            def link(ins):
                steps[0] += 1
                ins.then_inc(pool_step, 1)
                pool.wait_ge(pool_step, steps[0])

            def rsqrt(k):
                pool.wait_ge(var_ready, k + 1)
                pool.tensor_tensor(rstd[:, :], vare[:, :], half_neg[:, :], ALU.pow).then_inc(rstd_ready, 1)

            link(pool.memset(half_neg[:, :], -0.5))
            rsqrt(0)
            pool.memset(vaug[:, :, :, :, :], 0.0).then_inc(pool_step, 1)
            steps[0] += 1
            pool.memset(kst[:, :, :, :], 1.0).then_inc(vzero, 1)
            pool.wait_ge(pool_step, steps[0])
            v = vaug[:, :, :, :, :].rearrange("p a k (f j) c -> p (a k f) j c", j=2)
            for j in range(2):
                pool.memset(v[:, :, j, 16 * j + 8:16 * j + 9], 1.0).then_inc(vzero, 1)
            pool.wait_ge(loaded_w, 96)
            pool.tensor_copy(identb[:, :], ident).then_inc(consts_ready, 1)

            def split(b):
                for a in range(2):
                    pool.wait_ge(misc_free, pre_base(b) + 5 + 3 * a)
                    link(pool.tensor_tensor(rope[:, a, 2], rope[:, a, 2], rope[:, a, 1], ALU.add))
                    if b:
                        pool.wait_ge(parts_stored[b - 1], 64)
                    link(pool.tensor_copy(parts[:, a, 0], rope[:, a, 2]))
                    link(pool.tensor_tensor(rope[:, a, 1], rope[:, a, 2], parts[:, a, 0], ALU.subtract))
                    link(pool.tensor_copy(parts[:, a, 1], rope[:, a, 1]))
                    pool.tensor_tensor(parts[:, a, 2], rope[:, a, 1], parts[:, a, 1], ALU.subtract)\
                        .then_inc(parts_ready, 1)

            def residual(b):
                pool.wait_ge(loaded_x[b], 16)
                if b:
                    pool.wait_ge(misc_free, post_base(b - 1) + 4)
                pool.tensor_tensor(xbo[:, :, :], xin[:, b],
                                   rows_s[:, 128:256].unsqueeze(1).broadcast_to([P, NT, P]), ALU.add)\
                    .then_inc(xbo_ready, 1)

            k = 1
            for b in range(B + 2):
                if b < B:
                    if b:
                        rsqrt(k)
                        k += 1
                    split(b)
                if b == 0:
                    residual(0)
                if 2 <= b:
                    rsqrt(k)
                    k += 1
                    if b - 1 < B:
                        residual(b - 1)
            pool.wait_ge(loaded_ffn, 112)
            pool.tensor_copy(sel_s[:, :], selc_s[:, :]).then_inc(consts_ready, 1)

        @block.scalar
        def _(act):
            def pre_task(b, k):
                base = pre_base(b) + k + 1
                if k == 0:
                    act.wait_ge(misc_filled, base)
                    if b:
                        act.wait_ge(misc_free, base - 1)
                    nc.scalar.activation(xnT[:, :].rearrange("d (p i) -> d i p", i=NT),
                                         misc[:, :].rearrange("d (i p) -> d i p", i=NT), ACT.Copy)\
                        .then_inc(misc_free, 1)
                if k == 1:
                    act.wait_ge(misc_filled, base)
                    nc.scalar.activation(ctT[:, :], misc[:, :], ACT.Identity, bias=cols_s[:, CBD:CBD + 1])\
                        .then_inc(misc_free, 1)

            def post_task(b, k):
                base = post_base(b) + k + 1
                if k == 2:
                    act.wait_ge(misc_filled, base)
                    nc.scalar.activation(otT[:, :, :], misc[:, :], ACT.Copy).then_inc(misc_free, 1)
                if k == 4:
                    act.wait_ge(misc_filled, base)
                    nc.scalar.activation(x2T[:, S * b:S * b + S].rearrange("d (p i) -> d i p", i=NT),
                                         misc[:, :].rearrange("d (i p) -> d i p", i=NT), ACT.Copy)\
                        .then_inc(misc_free, 1)
                if k == 6:
                    act.wait_ge(misc_filled, base)
                    nc.scalar.activation(scT[:, RUN * b:RUN * b + RUN], misc[:, 0:RUN], ACT.Copy)\
                        .then_inc(misc_free, 1)

            def router_exp(b):
                act.wait_ge(logits_ready, b + 1)
                nc.scalar.activation(sc[:, :, :], sc[:, :, :], ACT.Exp).then_inc(rexp_ready, 1)

            def ffn_out(blk):
                act.wait_ge(down_done, NE * (blk + 1))
                if blk:
                    act.wait_ge(yt_filled, blk)
                nc.scalar.activation(yT, obank[:, :], ACT.Copy).then_inc(yT_ready, 1)

            for dst, src in ((trig_s[:, 0:KCOS], trig[:, 0:KCOS]), (wa_s[:, :], wa), (cols_s[:, :], cols), (wb_s[:, :], wb)):
                act.dma_start(dst, src).then_inc(loaded_w, 16)
            act.wait_ge(loaded_w, 96)
            for k in range(2):
                pre_task(0, k)
            for n in range(SLOTS + 64):
                u = (n - ST_LAG) // 2
                if (n - ST_LAG) % 2 == 0 and 0 <= u < UQ * NQUAD:
                    act.wait_ge(st_filled, u + 1)
                    if u >= PT:
                        act.wait_ge(pv_done, (u - PT) // 2 + 1)
                    nc.scalar.activation(pt[:, u % PT], stp[:, u % 2], ACT.Exp, scale=SCALE)\
                        .then_inc(exp_done, 1)
                if (n - ST_LAG) % 2 == 0 and u % UQ == 2 and (u // UQ) % 2 == 0 and 0 < u // UQ <= NQUAD:
                    g = u // UQ - 1
                    s = (g % NQ) // 2
                    act.wait_ge(pv_done, NT * (g + 1))
                    if g >= NQ:
                        act.wait_ge(misc_filled, post_base(g // NQ - 1) + s + 1)
                    nc.scalar.activation(osb[:, s], obank[:, :], ACT.Copy).then_inc(o_out, 1)
                for b in range(1, B):
                    for k in range(2):
                        if n == pre_slot(b, k):
                            pre_task(b, k)
                for b in range(B):
                    for k in (2, 4, 6):
                        if n == post_slot(b, k):
                            post_task(b, k)
                    if n == post_slot(b, 5) + 2:
                        router_exp(b)
            act.wait_ge(loaded_ffn, 112)
            for t in range(B * NE):
                n = t % NE
                act.wait_ge(up_filled, t + 1)
                if t >= 2:
                    act.wait_ge(u_done, t - 1)
                nc.scalar.activation(act_s[:, t % 2], bank[t % 2][:, :], ACT.Silu,
                                     bias=cols_s[:, CUP + n:CUP + n + 1]).then_inc(silu_done, 1)
                if t % NE == 1 and t > NE:
                    ffn_out(t // NE - 1)
            ffn_out(B - 1)

        @block.tensor
        def _(pe):
            def tile_w(c):
                return wa_s[:, c:c + P]

            def pre_task(b, k):
                base = pre_base(b) + k
                if base:
                    pe.wait_ge(misc_free, base)
                if k == 0:
                    pe.wait_ge(xn_ready, b + 1)
                    for i in range(NT):
                        last = nc.tensor.transpose(misc[:, P * i:P * i + P], xn[:, i], ident)
                elif k == 1:
                    last = nc.tensor.matmul(misc[:, :], tile_w(WD), xnT[:, :], start=True, stop=True)
                elif k in (2, 3, 4):
                    c = (WQR, WQRS, WUQ)[k - 2]
                    last = nc.tensor.matmul(misc[:, :], wb_s[0:64, c:c + P], ctT[0:64, :], start=True, stop=True)
                elif k in (5, 6):
                    last = nc.tensor.matmul(misc[:, :], tile_w((WKR, WKRS)[k - 5]), xnT[:, :], start=True, stop=True)
                elif k == 7:
                    last = nc.tensor.matmul(misc[:, :], wb_s[64:128, WUK:WUK + P], ctT[64:128, :],
                                            start=True, stop=True)
                else:
                    for i in range(NT):
                        last = nc.tensor.matmul(misc[:, P * i:P * i + P], ctT[64:128, P * i:P * i + P],
                                                wb_s[64:128, WUV:WUV + P], start=True, stop=True)
                last.then_inc(misc_filled, 1)

            def post_task(b, k):
                pe.wait_ge(misc_free, post_base(b) + k)
                if k in (0, 1):
                    pe.wait_ge(o_out, 2 * b + k + 1)
                    for i in range(NT):
                        last = nc.tensor.transpose(misc[:, P * i:P * i + P], osb[:, k, i::NT], ident)
                elif k == 2:
                    for i in range(NT):
                        last = nc.tensor.transpose(misc[:, P * i:P * i + P], ot[:, i], ident)
                elif k == 3:
                    for i in range(NT):
                        last = nc.tensor.matmul(misc[:, P * i:P * i + P], otT[:, i], tile_w(WO), start=True, stop=True)
                elif k == 4:
                    pe.wait_ge(xn2_ready, b + 1)
                    for i in range(NT):
                        last = nc.tensor.transpose(misc[:, P * i:P * i + P], xn[:, i], ident)
                elif k == 5:
                    for i in range(NT):
                        c = S * b + P * i
                        last = nc.tensor.matmul(misc[:, E * i:E * i + E], x2T[:, c:c + P], wa_s[:, WR:WR + E],
                                                start=True, stop=True)
                else:
                    pe.wait_ge(sc_ready, b + 1)
                    for i in range(NT):
                        r, c = 64 * (i // 2), P * (i % 2)
                        last = nc.tensor.matmul(misc[r:r + 64, c:c + P], sc[:, i], ident, start=True, stop=True)
                last.then_inc(misc_filled, 1)

            def nat(n):
                g, i = divmod(n, 16)
                b, q = divmod(g, NQ)
                t, g1, hp = i // 4, i // 2 % 2, i % 2
                if i == 0 and q == 0:
                    pe.wait_ge(stacks_ready[b % 2], 16 * 18 * (b // 2 + 1))
                use = nat_use(n)
                if use >= 2:
                    pe.wait_ge(nat_free, use - 1)
                r, h = 64 * hp, h2(q, g1)
                nc.tensor.matmul(bank[use % 2][:, :], qst[r:r + QROWS, b % 2, h, P * t:P * t + P],
                                 kst[r:r + QROWS, b % 2, h, :], start=True, stop=True).then_inc(nat_filled, 1)

            def max_rows(g):
                use = mt_use(g)
                pe.wait_ge(nat_free, use - 1)
                pe.wait_ge(mparts_ready, g + 1)
                o = bank[use % 2][0:4 * MROWS, 0:S // 2].bitcast(BF16)
                for t in range(NT):
                    last = nc.tensor.transpose(o[:, P * t:P * t + P],
                                               mpart[:, g % 2, t].rearrange("p a b -> p (a b)"), identb[:, :])
                last.then_inc(nat_filled, 1)

            def scores(u):
                g, k = divmod(u, UQ)
                b, q = divmod(g, NQ)
                kt, g1 = divmod(k, 2)
                if k == 0:
                    pe.wait_ge(mrows_ready[g % 2], 16 * 2 * MROWS * (g // 2 + 1))
                if u >= 2:
                    pe.wait_ge(exp_done, u - 1)
                h = h2(q, g1)
                for hp in range(2):
                    r = 64 * hp
                    last = nc.tensor.matmul(stp[:, u % 2, hp], kst[r:r + KST, b % 2, h, P * kt:P * kt + P],
                                            qst[r:r + KST, b % 2, h, :], start=True, stop=True)
                last.then_inc(st_filled, 1)

            def weigh(v):
                g, kt = divmod(v, NT)
                b, q = divmod(g, NQ)
                j = q % 2
                pe.wait_ge(exp_done, 2 * v + 2)
                if kt == 0:
                    pe.wait_ge(misc_free, pre_base(b) + NPRE)
                if kt == 0 and j == 0 and g:
                    pe.wait_ge(o_out, g // 2)
                for hp in range(2):
                    for g1 in range(2):
                        c = 32 * (2 * hp + g1)
                        last = nc.tensor.matmul(obank[c:c + 32, :], vaug[:, b % 2, kt, 8 * hp + h2(q, g1)],
                                                pt[:, (2 * v + g1) % PT, hp], start=(j == 0 and kt == 0),
                                                stop=(j == 1 and kt == NT - 1), tile_position=(0, c))
                last.then_inc(pv_done, 1)

            pe.wait_ge(loaded_w, 96)
            pe.wait_ge(consts_ready, 1)
            for k in range(NPRE):
                pre_task(0, k)
            pe.wait_ge(vzero, 3)
            for n in range(SLOTS + 64):
                if n < 16 * NQUAD:
                    nat(n)
                if n >= 16 and n % 16 == 3 and n // 16 <= NQUAD:
                    max_rows(n // 16 - 1)
                if (n - ST_LAG) % 2 == 0 and n >= ST_LAG:
                    u = (n - ST_LAG) // 2
                    if u < UQ * NQUAD:
                        scores(u)
                    if u >= PV_LAG and (u - PV_LAG) % 4 == 0 and u - PV_LAG < UQ * NQUAD:
                        weigh((u - PV_LAG) // 2)
                        weigh((u - PV_LAG) // 2 + 1)
                for b in range(1, B):
                    for k in range(NPRE):
                        if n == pre_slot(b, k):
                            pre_task(b, k)
                for b in range(B):
                    for k in range(NPOST):
                        if n == post_slot(b, k):
                            post_task(b, k)

            def summed(k, jobs):
                pe.wait_ge(rmat_in, k + 1)
                for c, w, mat, rhs in jobs:
                    last = nc.tensor.matmul(misc[:, c:c + w], cst_s[:, mat:mat + P], rhs, start=True, stop=True)
                last.then_inc(rmat_out, 1)

            for s in range(DIGITS):
                summed(s, [(0, 16, KONE, cnt[:, :])])
            summed(DIGITS, [(0, 1, KONE, one[:, 0:1]), (1, NB, KTRI, eq[:, :]), (17, NB, KBLK, eq[:, :]),
                            (33, 1, KH01, one[:, 1:2])])
            pe.wait_ge(rmat_in, DIGITS + 2)
            nc.tensor.transpose(misc[0:1, 0:P], one[:, 4:5], ident).then_inc(rmat_out, 1)
            pe.wait_ge(rmat_in, DIGITS + 3)
            nc.tensor.transpose(misc[:, P:P + 1], trow[0:1, P:2 * P], ident[0:1, 0:1]).then_inc(rmat_out, 1)
            summed(DIGITS + 3, [(0, 2, KPAIR, one[:, 6:8]), (2, B, KOTHER, eqc[:, :]), (2 + B, B, KNEXT, eqc[:, :])])
            pe.wait_ge(fsp_ready, 3)
            for k in range(B * NT):
                b, i = divmod(k, NT)
                for half in range(2):
                    r = 64 * half
                    last = nc.tensor.matmul(misc[r:r + 64, k:k + 1], ping[0][:, RUN * b + i:RUN * b + RUN:NT],
                                            cst_s[:, KBLK + r:KBLK + r + 1], start=True, stop=True)
            last.then_inc(den_done, 1)

            pe.wait_ge(loaded_ffn, 112)
            pe.wait_ge(consts_ready, 2)
            pe.wait_ge(fs_ready, 16 * 14)

            def down(t):
                blk, n = divmod(t, NE)
                pe.wait_ge(h_done, t + 1)
                if n == 0:
                    if blk:
                        pe.wait_ge(yT_ready, blk)
                    nc.tensor.matmul(obank[:, :], bdown_s[:, :], msf[:, S * blk:S * blk + S], start=True, stop=False)
                nc.tensor.matmul(obank[:, :], wdown_s[:, n], h_s[:, t % 3], start=False, stop=n == NE - 1)\
                    .then_inc(down_done, 1)

            def back(blk):
                pe.wait_ge(yT_ready, blk + 1)
                pe.wait_ge(y_ready, blk + 0) if blk else pe.wait_ge(den_done, 1)
                for i in range(NT):
                    last = nc.tensor.transpose(misc[:, P * i:P * i + P], vaug_f[:, 7, i::NT], ident)
                last.then_inc(yt_filled, 1)

            for t in range(B * NE):
                blk, n = divmod(t, NE)
                xb = x2T[:, S * blk:S * blk + S]
                if t >= 2:
                    pe.wait_ge(silu_done, t - 1)
                nc.tensor.matmul(bank[t % 2][:, :], wup_s[:, P * n:P * n + P], xb, start=True, stop=True)\
                    .then_inc(up_filled, 1)
                if t >= 2:
                    pe.wait_ge(u_done, t - 1)
                nc.tensor.matmul(stp[:, 0, t % 2], wgate_s[:, P * n:P * n + P], xb, start=True, stop=True)\
                    .then_inc(gate_filled, 1)
                if t >= 2:
                    pe.wait_ge(h_done, t - 1)
                nc.tensor.matmul(stp[:, 1, t % 2], sel_s[:, P * (n % 8):P * (n % 8) + P],
                                 fs[:, n // 8, S * blk:S * blk + S], start=True, stop=True).then_inc(mask_filled, 1)
                if t >= 2:
                    down(t - 2)
                if n == 5 and blk:
                    back(blk - 1)
            down(B * NE - 2)
            down(B * NE - 1)
            back(B - 1)

        @block.vector
        def _(dve):
            steps = [0]
            V = nc.vector

            def link(ins):
                steps[0] += 1
                ins.then_inc(dve_step, 1)
                dve.wait_ge(dve_step, steps[0])

            def norm_stats(src):
                for i in range(NT):
                    last = V.bn_stats(stats[:, i], src[:, i])
                link(last)
                for i in range(NT):
                    last = V.bn_aggr(mv[:, i], stats[:, i])
                link(last)
                V.tensor_scalar(vare[:, :], mv[:, :, 1], EPS, None, ALU.add).then_inc(var_ready, 1)

            def norm_apply(src, k):
                dve.wait_ge(rstd_ready, k + 1)
                for i in range(NT):
                    last = V.tensor_scalar(xn[:, i], src[:, i], mv[:, i, 0:1], rstd[:, i:i + 1],
                                           ALU.subtract, ALU.mult)
                return last

            first_norm, second_norm = (0, 1, 2, 4), (3, 5, 6, 7)

            def pre_stats(b):
                dve.wait_ge(loaded_x[b], 16)
                norm_stats(xin[:, b])

            def pre_norm(b):
                norm_apply(xin[:, b], first_norm[b]).then_inc(xn_ready, 1)

            def pre_task(b, k):
                dve.wait_ge(misc_filled, pre_base(b) + k + 1)
                if k in (2, 3, 5, 6):
                    a, c = divmod(k - 2, 3)
                    if b:
                        dve.wait_ge(parts_ready, 2 * (b - 1) + a + 1)
                    col = ((CAQ, CBQ), (CAK, CBK))[a][c]
                    V.scalar_tensor_tensor(out=rope[:, a, c], in0=misc[:, :], scalar=cols_s[:, col:col + 1],
                                           in1=(cosT, sinT)[c], op0=ALU.add, op1=ALU.mult).then_inc(misc_free, 1)
                elif k in (4, 7):
                    a = (k - 4) // 3
                    col = (CCQ, CCK)[a]
                    dve.wait_ge(misc_free, pre_base(b) + k)
                    V.scalar_tensor_tensor(out=rope[:, a, 2], in0=misc[:, :], scalar=cols_s[:, col:col + 1],
                                           in1=rope[:, a, 0], op0=ALU.add, op1=ALU.add).then_inc(misc_free, 1)
                elif k == 8:
                    dve.wait_ge(vzero, 3)
                    if b >= 2:
                        dve.wait_ge(pv_done, NT * NQ * (b - 1))
                    m = misc[:, :].rearrange("p (k f j d) -> p (k f) j d", k=NT, j=2, d=HD)
                    bv = rows_s[:, 0:128].rearrange("p (f j d) -> p f j d", j=2, d=HD)
                    vv = vaug[:, b % 2].rearrange("p k (f j) c -> p k f j c", j=2)
                    mm = misc[:, :].rearrange("p (k f j d) -> p k f j d", k=NT, j=2, d=HD)
                    for j in range(2):
                        last = V.tensor_tensor(vv[:, :, :, j, 16 * j:16 * j + HD], mm[:, :, :, j, :],
                                               bv[:, :, j, :].unsqueeze(1).broadcast_to([P, NT, H // 2, HD]), ALU.add)
                        if j == 0:
                            link(last)
                    last.then_inc(misc_free, 1)

            def post_task(b, k):
                if k in (0, 1, 3, 5):
                    dve.wait_ge(misc_filled, post_base(b) + k + 1)
                if k in (0, 1):
                    m = misc[:, :].rearrange("p (r c) -> p r c", c=16)
                    link(V.reciprocal(rden[:, k], m[:, :, 8]))
                    V.tensor_tensor(ot[:, :, 64 * k:64 * k + 64].rearrange("p i (r d) -> p i r d", d=HD),
                                    misc[:, :].rearrange("p (i r c) -> p i r c", i=NT, c=16)[:, :, :, 0:HD],
                                    rden[:, k].rearrange("p (i r) -> p i r", i=NT)
                                    .unsqueeze(3).broadcast_to([P, NT, 8, HD]), ALU.mult).then_inc(misc_free, 1)
                elif k == 3:
                    dve.wait_ge(xbo_ready, b + 1)
                    V.tensor_tensor(x2[:, b], misc[:, :].rearrange("p (i d) -> p i d", d=P), xbo[:, :, :], ALU.add)\
                        .then_inc(misc_free, 1)
                    dve.wait_ge(misc_free, post_base(b) + k + 1)
                    norm_stats(x2[:, b])
                elif k == 5:
                    V.tensor_tensor(sc[:, :, :], misc[:, 0:NT * E].rearrange("p (i e) -> p i e", e=E),
                                    rows_s[:, 256:320].unsqueeze(1).broadcast_to([P, NT, E]), ALU.add)\
                        .then_inc(misc_free, 1)
                    dve.wait_ge(misc_free, post_base(b) + k + 1)
                    link(V.tensor_reduce(srow[:, 0], sc[:, :, :], AX, ALU.max))
                    V.tensor_tensor(sc[:, :, :], sc[:, :, :], srow[:, 0].unsqueeze(2).broadcast_to([P, NT, E]),
                                    ALU.subtract).then_inc(logits_ready, 1)

            def router_norm(b):
                dve.wait_ge(rexp_ready, b + 1)
                link(V.tensor_reduce(srow[:, 1], sc[:, :, :], AX, ALU.add))
                link(V.reciprocal(srow[:, 2], srow[:, 1]))
                V.tensor_tensor(sc[:, :, :], sc[:, :, :], srow[:, 2].unsqueeze(2).broadcast_to([P, NT, E]),
                                ALU.mult).then_inc(sc_ready, 1)

            def row_max(n):
                g, i = divmod(n, 16)
                t, c = i // 4, 2 * (i % 2) + i // 2 % 2
                use = nat_use(n)
                dve.wait_ge(nat_filled, use + 1)
                V.tensor_reduce(mx[:, g % 2, t, c:c + 1], bank[use % 2][:, :], AX, ALU.max).then_inc(nat_free, 1)

            def max_parts(g):
                dve.wait_ge(nat_free, nat_use(16 * g + 15) + 1)
                if g >= 2:
                    dve.wait_ge(nat_filled, mt_use(g - 2) + 1)
                m = mx[:, g % 2]
                link(V.tensor_scalar(mpart[:, g % 2, :, 0], m, -1.0, None, ALU.mult))
                V.scalar_tensor_tensor(out=mpart[:, g % 2, :, 1], in0=m, scalar=-1.0, in1=mpart[:, g % 2, :, 0],
                                       op0=ALU.mult, op1=ALU.subtract).then_inc(mparts_ready, 1)

            def max_rows(g):
                use = mt_use(g)
                dve.wait_ge(nat_filled, use + 1)
                if g >= 2:
                    dve.wait_ge(mrows_ready[g % 2], 32 * MROWS * (g // 2))
                V.tensor_copy(mts[:, g % 2, :], bank[use % 2][0:4 * MROWS, 0:S // 2].bitcast(BF16))\
                    .then_inc(nat_free, 1)

            def exchange(top_d, low_d, top_s, low_s):
                V.tensor_tensor(top_d, top_s, low_s, ALU.max)
                link(V.tensor_tensor(low_d, top_s, low_s, ALU.min))

            def sort_stage(k, c0, c1):
                m, d = SORT[k]
                src, dst = (scT if k == 0 else ping[(k - 1) % 2])[:, c0:c1], ping[k % 2][:, c0:c1]
                if d == 0:
                    s_, d_ = (t.rearrange("p (n m) -> p n m", m=m) for t in (src, dst))
                    stop = m // 2 - 1 if m > 2 else 0
                    if m == 2:
                        exchange(d_[:, :, 0:1], d_[:, :, 1:2], s_[:, :, 0:1], s_[:, :, 1:2])
                    else:
                        exchange(d_[:, :, 0:m // 2], d_[:, :, m - 1:stop:-1], s_[:, :, 0:m // 2], s_[:, :, m - 1:stop:-1])
                else:
                    s_, d_ = (t.rearrange("p (n a k) -> p n a k", a=2, k=d) for t in (src, dst))
                    exchange(d_[:, :, 0], d_[:, :, 1], s_[:, :, 0], s_[:, :, 1])

            def sort_b(b, ks):
                dve.wait_ge(misc_free, post_base(b) + NPOST)
                for k in ks:
                    sort_stage(k, RUN * b, RUN * b + RUN)

            def merge(b2, ks):
                for k in ks:
                    sort_stage(k, S * (b2 - 1), S * b2)

            pre_stats(0)
            pre_norm(0)
            dve.wait_ge(loaded_w, 96)
            for k in range(2, NPRE):
                pre_task(0, k)
            for n in range(SLOTS + 64):
                if n < 16 * NQUAD:
                    row_max(n)
                if n % 16 == 15 and n // 16 < NQUAD:
                    max_parts(n // 16)
                if n >= 16 and n % 16 == 3 and n // 16 <= NQUAD:
                    max_rows(n // 16 - 1)
                for b in range(B - 1):
                    k = n - 64 * (b + 2)
                    if 0 <= k < STAGES_RUN:
                        sort_b(b, [k])
                if 0 <= n - 64 * 3 - STAGES_RUN < STAGES_PAIR - STAGES_RUN:
                    merge(1, [n - 64 * 3])
                for b in range(1, B):
                    if n == pre_slot(b, 0) - 2:
                        pre_stats(b)
                    if n == pre_slot(b, 0) - 1:
                        pre_norm(b)
                    for k in range(2, NPRE):
                        if n == pre_slot(b, k):
                            pre_task(b, k)
                for b in range(B):
                    for k in range(NPOST):
                        if n == post_slot(b, k):
                            post_task(b, k)
                    if n == post_slot(b, 3) + 3:
                        norm_apply(x2[:, b], second_norm[b]).then_inc(xn2_ready, 1)
                    if n == post_slot(b, 5) + 4:
                        router_norm(b)

            sort_b(B - 1, range(STAGES_RUN))
            merge(B // 2, range(STAGES_RUN, STAGES_PAIR))
            for k in range(STAGES_PAIR, len(SORT)):
                sort_stage(k, 0, HALF)
            V.engine_nop().then_inc(swap_in, 1)
            dve.wait_ge(swapped, 32)
            V.tensor_tensor(ping[1][0:64, :], ping[0][0:64, :], other[0:64, ::-1], ALU.max)
            link(V.tensor_tensor(ping[1][64:128, :], other[64:128, :], ping[0][64:128, ::-1], ALU.min))
            src, side = ping[1], 0
            k = HALF // 2
            while k >= GRP:
                dst = ping[side]
                s_, d_ = (t[:, :].rearrange("p (n a k) -> p n a k", a=2, k=k) for t in (src, dst))
                exchange(d_[:, :, 0], d_[:, :, 1], s_[:, :, 0], s_[:, :, 1])
                src, side = dst, 1 - side
                k //= 2
            blocks = src[:, :].rearrange("p (n k) -> p n k", k=GRP)
            V.tensor_reduce(gsum[:, :], blocks, AX, ALU.add)
            V.tensor_reduce(gmin[:, :], blocks, AX, ALU.min)

            link(V.memset(prefix[:, :], 0))
            dve.wait_ge(loaded_ffn, 112)
            asks = [0]

            def ask():
                asks[0] += 1
                V.engine_nop().then_inc(rmat_in, 1)
                dve.wait_ge(rmat_out, asks[0])

            for s in range(DIGITS):
                link(V.tensor_tensor(cand[:, :], kdig_s[:, s], prefix[:, :].broadcast_to([P, 16]), ALU.bitwise_or))
                link(V.tensor_tensor(ge[:, :, :], gsum[:, :].unsqueeze(1).broadcast_to([P, 16, NB]),
                                     cand[:, :].bitcast(F32).unsqueeze(2).broadcast_to([P, 16, NB]), ALU.is_ge))
                link(V.tensor_reduce(cnt[:, :], ge[:, :, :], AX, ALU.add))
                ask()
                link(V.scalar_tensor_tensor(out=pick[:, :], in0=misc[:, 0:16], scalar=float(BUDGET),
                                            in1=cand[:, :].bitcast(F32), op0=ALU.is_ge, op1=ALU.mult))
                link(V.tensor_reduce(prefix[:, :].bitcast(F32), pick[:, :], AX, ALU.max))
            least = prefix[:, :].bitcast(F32)
            V.tensor_scalar(gt[:, :], gsum[:, :], least, None, ALU.is_gt, ALU.add, accum_out=one[:, 0:1])
            link(V.tensor_scalar(eq[:, :], gsum[:, :], least, None, ALU.is_equal, ALU.add, accum_out=one[:, 1:2]))
            ask()
            link(V.tensor_copy(rt[:, 0:34], misc[:, 0:34]))
            V.tensor_scalar(one[:, 2:3], rt[:, 0:1], -1.0, float(BUDGET), ALU.mult, ALU.add)
            link(V.tensor_tensor_scan(gr[:, 0], rt[:, 17:33], rt[:, 17:33], 0.0, ALU.add, ALU.max))
            link(V.scalar_tensor_tensor(out=gr[:, 1], in0=gr[:, 0], scalar=rt[:, 33:34], in1=rt[:, 1:17],
                                        op0=ALU.add, op1=ALU.add))
            link(V.tensor_tensor(gr[:, 2], gr[:, 1], rt[:, 17:33], ALU.subtract))
            link(V.scalar_tensor_tensor(out=gr[:, 3], in0=gr[:, 2], scalar=one[:, 2:3], in1=eq[:, :],
                                        op0=ALU.is_lt, op1=ALU.mult))
            link(V.tensor_tensor(gr[:, 4], gr[:, 3], gt[:, :], ALU.add))
            V.tensor_reduce(one[:, 7:8], gr[:, 4], AX, ALU.add)
            link(V.tensor_scalar(gr[:, 5], gr[:, 4], -3.0, 3.0, ALU.mult, ALU.add))
            link(V.tensor_tensor(gr[:, 0], gr[:, 5], gmin[:, :], ALU.max))
            link(V.tensor_reduce(one[:, 4:5], gr[:, 0], AX, ALU.min))
            ask()
            link(V.tensor_copy(trow[:, 0:P], misc[0:1, 0:P]))
            for k in range(2):
                last = V.tensor_tensor(trow[:, P + E * k:P + E * k + E], trow[:, 0:E], trow[:, E:P], ALU.min)
            link(last)
            ask()
            link(V.tensor_copy(one[:, 5:6], misc[:, P:P + 1]))
            V.tensor_scalar(ping[0][:, :], scT[:, :], one[:, 5:6], None, ALU.is_gt, ALU.add, accum_out=one[:, 6:7])
            link(V.tensor_scalar(ping[1][:, :], scT[:, :], one[:, 5:6], None, ALU.is_equal))
            link(V.tensor_reduce(eqc[:, :], ping[1][:, :].rearrange("p (b t) -> p b t", b=B), AX, ALU.add))
            ask()
            link(V.tensor_copy(rt[:, 0:2 + 2 * B], misc[:, 0:2 + 2 * B]))
            link(V.scalar_tensor_tensor(out=one[:, 9:10], in0=rt[:, 1:2], scalar=float(GRP), in1=rt[:, 0:1],
                                        op0=ALU.mult, op1=ALU.subtract))
            link(V.tensor_tensor_scan(eqo[:, 0], rt[:, 2:2 + B], rt[:, 2:2 + B], 0.0, ALU.add, ALU.max))
            link(V.tensor_tensor(eqo[:, 1], eqo[:, 0], rt[:, 2 + B:2 + 2 * B], ALU.subtract))
            link(V.tensor_tensor_scan(other[:, :], ping[1][:, :], ping[1][:, :], 0.0, ALU.add, ALU.max))
            o_ = other[:, :].rearrange("p (b t) -> p b t", b=B)
            link(V.tensor_tensor(o_, o_, eqo[:, 1].unsqueeze(2).broadcast_to([P, B, RUN]), ALU.add))
            link(V.scalar_tensor_tensor(out=other[:, :], in0=other[:, :], scalar=one[:, 9:10], in1=ping[1][:, :],
                                        op0=ALU.is_le, op1=ALU.mult))
            link(V.tensor_tensor(ping[0][:, :], ping[0][:, :], other[:, :], ALU.add))
            link(V.tensor_tensor(ping[0][:, :], ping[0][:, :], scT[:, :], ALU.mult))
            V.engine_nop().then_inc(fsp_ready, 1)
            link(V.tensor_copy(fsp[:, 0], ping[0][:, :]))
            link(V.tensor_tensor(ping[1][:, :], ping[0][:, :], fsp[:, 0], ALU.subtract))
            link(V.tensor_copy(fsp[:, 1], ping[1][:, :]))
            V.engine_nop().then_inc(fsp_ready, 1)
            V.tensor_tensor(fsp[:, 2], ping[1][:, :], fsp[:, 1], ALU.subtract).then_inc(fsp_ready, 1)
            dve.wait_ge(den_done, 1)
            link(V.tensor_scalar(rtok[:, :], misc[:, 0:NT * B], 1e-6, None, ALU.add))
            link(V.reciprocal(rtok[:, :], rtok[:, :]))

            def finish(blk):
                dve.wait_ge(yt_filled, blk + 1)
                if blk >= 2:
                    dve.wait_ge(stored[blk % 2], 16 * (blk // 2))
                for i in range(NT):
                    k = NT * blk + i
                    last = V.scalar_tensor_tensor(out=y_s[:, blk % 2, i], in0=misc[:, P * i:P * i + P],
                                                  scalar=rtok[:, k:k + 1], in1=x2[:, blk, i],
                                                  op0=ALU.mult, op1=ALU.add)
                last.then_inc(y_ready, 1)

            for t in range(B * NE):
                blk, n = divmod(t, NE)
                dve.wait_ge(gate_filled, t + 1)
                dve.wait_ge(silu_done, t + 1)
                if t >= 2:
                    dve.wait_ge(h_done, t - 1)
                V.scalar_tensor_tensor(out=u_s[:, t % 2], in0=stp[:, 0, t % 2], scalar=cols_s[:, CGT + n:CGT + n + 1],
                                       in1=act_s[:, t % 2], op0=ALU.add, op1=ALU.mult).then_inc(u_done, 1)
                dve.wait_ge(mask_filled, t + 1)
                dve.wait_ge(u_done, t + 1)
                if t >= 3:
                    dve.wait_ge(down_done, t - 2)
                V.tensor_tensor(h_s[:, t % 3], stp[:, 1, t % 2], u_s[:, t % 2], ALU.mult).then_inc(h_done, 1)
                if n == 6 and blk:
                    finish(blk - 1)
            finish(B - 1)
    return nc


def kernel(**inputs):
    import numpy as np
    import concourse.bacc as bacc
    from concourse.bass_utils import run_bass_kernel_spmd as run

    f = {k: np.asarray(v) for k, v in inputs.items()}
    a = {k[8:]: v for k, v in f.items() if k.startswith("L0_attn_")}
    m = {k[7:]: v for k, v in f.items() if k.startswith("L0_ffn_")}
    order = np.arange(D).reshape(2, 8, HD).transpose(0, 2, 1).reshape(-1)
    swap = order ^ 1
    worder = np.arange(D).reshape(2, 2, 2, 2, HD).transpose(1, 0, 2, 3, 4).reshape(-1)
    wa = np.concatenate([a["Wd_q_w"], a["Wd_kv_w"], a["Wk_r_w"][:, order], a["Wk_r_w"][:, swap],
                         m["Wr"], a["Wo_w"][worder]], axis=1)
    wb = np.concatenate([np.concatenate([a["Wu_q_w"][:, order], a["Wq_r_w"][:, order], a["Wq_r_w"][:, swap]], axis=1),
                         np.concatenate([a["Wu_k_w"][:, order], a["Wu_v_w"], np.zeros((LAT, D), np.float32)], axis=1)])
    cols = np.concatenate([np.concatenate([a["Wd_q_b"], a["Wd_kv_b"]])[:, None],
                           a["Wu_q_b"][order][:, None], a["Wq_r_b"][order][:, None], a["Wq_r_b"][swap][:, None],
                           a["Wu_k_b"][order][:, None], a["Wk_r_b"][order][:, None], a["Wk_r_b"][swap][:, None],
                           m["bup"].reshape(NE, P).T, m["bgate"].reshape(NE, P).T], axis=1)
    rows = np.concatenate([a["Wu_v_b"], a["Wo_b"], m["br"]])[None]
    wup = m["Wup"].transpose(1, 0, 2).reshape(D, E * HE)
    wgate = m["Wgate"].transpose(1, 0, 2).reshape(D, E * HE)
    wdown = m["Wdown"].reshape(NE, P, D).transpose(1, 0, 2).reshape(P, NE * D)

    one = np.float32(1)
    ids = np.arange(D // 2, dtype=np.float32)
    theta = np.power(np.float32(10000.0), np.float32(-2.0) * ids) / np.float32(D // 2)
    angle = np.arange(S, dtype=np.float32)[:, None] * theta[None, :]
    cos, sin = np.cos(angle).T, np.sin(angle).T
    sign = np.where(order % 2 == 0, -one, one)[:, None]
    p = np.arange(P)
    half, ex = p // E, p % E
    same = half[:, None] == half[None, :]
    trig = np.concatenate([np.eye(P, dtype=np.float32), cos[order // 2], sin[order // 2] * sign], axis=1)
    cst = np.concatenate([
        (same & (ex[:, None] < ex[None, :])), same, (half[:, None] < half[None, :]),
        (ex[:, None] == ex[None, :]), (ex[:, None] == ex[None, :]) & ~same,
        (ex[:, None] == ex[None, :]) & (half[:, None] > half[None, :]),
        np.ones((P, P))], axis=1).astype(np.float32)
    selc = np.zeros((3, 32, 8, EPT, HE), np.float32)
    for n in range(8):
        for e in range(EPT):
            selc[:, EPT * n + e, n, e, :] = 1
    selc = selc.reshape(96, 8 * P)
    kdig = np.array([[k << (4 * (DIGITS - 1 - s)) for k in range(8 if s == 0 else 16)] + [0] * (8 if s == 0 else 0)
                     for s in range(DIGITS)], np.int32)
    kdig = np.broadcast_to(kdig.reshape(1, -1), (P, DIGITS * 16))

    arrays = dict(x=f["L0_attn_x"], wa=wa, wb=wb, cols=cols, rows=rows, wup=wup, wgate=wgate, wdown=wdown,
                  bdown=m["bdown"], trig=trig, cst=cst, selc=selc, kdig=kdig)
    arrays = {k: np.ascontiguousarray(v) for k, v in arrays.items()}
    nc = bacc.Bacc("TRN2", target_bir_lowering=False, num_devices=1)
    args = [nc.dram_tensor(k, v.shape, mybir.dt.from_np(v.dtype), kind="ExternalInput").ap() for k, v in arrays.items()]
    out = nc.dram_tensor("out", (B, S, D), F32, kind="ExternalOutput").ap()
    build(nc, *args, out)
    r = run(nc, [arrays], core_ids=[0])
    return r.results[0]["out"]
```

```python
from contextlib import ExitStack

import concourse.bass as bass
from concourse import mybir

F32 = mybir.dt.float32
BF16 = mybir.dt.bfloat16
I32 = mybir.dt.int32
ALU = mybir.AluOpType
ACT = mybir.ActivationFunctionType
AX = mybir.AxisListType.X

P = 128
B, S, D = 4, 512, 128
NT = S // P
H, HD = 16, 8
LAT = 64
E, HE = 64, 32
GRP, TOPK = 64, 16
TOK = B * S
BUDGET = TOK // GRP * TOPK
HALF = TOK // 2
NB = HALF // GRP
RUN = S // 2
NE = E * HE // P
EPT = P // HE
SCALE = 1.0 / float(H + LAT + LAT) ** 0.5
EPS = 1e-5
QROWS = 48
MROWS = 2
KST = QROWS + MROWS
NPRE, NPOST = 9, 7
NQ = 4
UQ = 2 * NT
NQUAD = B * NQ
ST_LAG = 28
PV_LAG = 5
PT = 8
SORT = [(m, d) for m in (2 ** k for k in range(1, 11)) for d in [0] + [m >> j for j in range(2, 11) if m >> j]]
STAGES_RUN = sum(m <= 256 for m, _ in SORT)
STAGES_PAIR = sum(m <= 512 for m, _ in SORT)
SLOTS = 16 * NQUAD + ST_LAG + 2 * PV_LAG + 2
EARLY = 3 * NE
EARLY_FIRST, EARLY_DIGIT, EARLY_COUNT = 32, 1, 2
DIRECT = 5
DIGITS = 8

WD, WKR, WKRS, WR, WO = 0, 128, 256, 384, 448
WUQ, WQR, WQRS = 0, 128, 256
WUK, WUV = 0, 128
CBD, CCQ, CAQ, CBQ, CCK, CAK, CBK, CUP, CGT = 0, 1, 2, 3, 4, 5, 6, 7, 23
KID, KCOS, KSIN = 0, 128, 640
KTRI, KBLK, KBELOW, KPAIR, KOTHER, KNEXT, KONE = 0, 128, 256, 384, 512, 640, 768
KEND = 896


def pre_base(b):
    return b * NPRE + max(b - 2, 0) * NPOST


def post_base(b):
    return min(b + 3, B) * NPRE + b * NPOST


def pre_slot(b, k):
    return 64 * (b - 1) + 8 + 3 * k if b else k - NPRE


POST_AT = [34, 37, 40, 43, 51, 54, 61]


def post_slot(b, k):
    return 64 * (b + 1) + POST_AT[k]


def nat_use(n):
    return n + max(0, (n + 12) // 16 - 1)


def mt_use(g):
    return min(16 * (g + 1) + 4, 16 * NQUAD) + g


def build(nc, x, wa, wb, cols, rows, wup, wgate, wdown, bdown, trig, cst, selc, kdig, out):
    ctx = ExitStack()
    with ctx:
        def sb(name, shape, dt=F32):
            return ctx.enter_context(nc.sbuf_tensor(name, shape, dt))

        def sem(name):
            return ctx.enter_context(nc.semaphore(name))

        parts_dram = nc.dram_tensor("parts_dram", (B, 2, 2, 3 * 8, 8 * S), BF16, kind="Internal").ap()

        wa_s = sb("wa_s", [P, 576])
        wb_s = sb("wb_s", [P, 384])
        cols_s = sb("cols_s", [P, 39])
        rows_s = sb("rows_s", [P, 320])
        wup_s = sb("wup_s", [P, NE * P])
        wgate_s = sb("wgate_s", [P, NE * P])
        wdown_s = sb("wdown_s", [P, NE, P])
        bdown_s = sb("bdown_s", [E, P])
        cst_s = sb("cst_s", [P, KEND])
        selc_s = sb("selc_s", [P, 8 * P])
        sel_s = sb("sel_s", [96, 8 * P], BF16)
        kdig_s = sb("kdig_s", [P, DIGITS, 16], I32)
        trig_s = sb("trig_s", [P, 1152])
        ident = trig_s[:, KID:KID + P]
        identb = sb("identb", [P, P], BF16)
        cosT, sinT = trig_s[:, KCOS:KCOS + S], trig_s[:, KSIN:KSIN + S]
        xin = sb("xin", [P, B, NT, P])
        xbo = sb("xbo", [P, NT, P])
        stats = sb("stats", [P, NT, 6])
        mv = sb("mv", [P, NT, 2])
        rstd = sb("rstd", [P, NT])
        vare = sb("vare", [P, NT])
        half_neg = sb("half_neg", [P, NT])
        xn = sb("xn", [P, NT, P])
        xnT = sb("xnT", [P, S])
        ctT = sb("ctT", [P, S])
        rope = sb("rope", [P, 2, 3, S])
        parts = sb("parts", [P, 2, 3, S], BF16)
        qst = sb("qst", [P, 2, 8, S], BF16)
        kst = sb("kst", [P, 2, 8, S], BF16)
        vaug = sb("vaug", [P, 2, NT, H, 32])
        mx = sb("mx", [P, 2, NT, 4])
        mpart = sb("mpart", [P, 2, NT, MROWS, 4], BF16)
        mts = sb("mts", [4 * MROWS, 2, S], BF16)
        pt = sb("pt", [P, PT, 2, S])
        osb = sb("osb", [P, 2, S])
        rden = sb("rden", [P, 2, NT * 8])
        ot = sb("ot", [P, NT, P])
        otT = sb("otT", [P, NT, P])
        x2 = sb("x2", [P, B, NT, P])
        x2T = sb("x2T", [P, TOK])
        sc = sb("sc", [P, NT, E])
        srow = sb("srow", [P, 3, NT])
        scT = sb("scT", [P, HALF])
        ping = [sb("ping0", [P, HALF]), sb("ping1", [P, HALF])]
        pt_f = pt[:, :, :, :].rearrange("p a b t -> p (a b t)")
        other = pt_f[:, 0:HALF]
        kst_f = kst[:, :, :, :].rearrange("p a h t -> p (a h t)")
        fsp = kst_f[:, 0:3 * HALF].rearrange("p (c t) -> p c t", c=3)
        msf = kst_f[0:E, 3 * HALF:3 * HALF + 2 * TOK].bitcast(F32)
        fs = qst[0:96, :, :, :].rearrange("p a h t -> p (a h t)")[:, 0:2 * TOK].rearrange("p (a t) -> p a t", a=2)
        gsum = sb("gsum", [P, NB])
        gmin = sb("gmin", [P, NB])
        cand = sb("cand", [P, 16], I32)
        ge = sb("ge", [P, 16, NB])
        cnt = sb("cnt", [P, 16])
        prefix = sb("prefix", [P, 1], I32)
        pick = sb("pick", [P, 16])
        gt = sb("gt", [P, NB])
        eq = sb("eq", [P, NB])
        gr = sb("gr", [P, 6, NB])
        one = sb("one", [P, 16])
        rt = sb("rt", [P, 40])
        eqc = sb("eqc", [P, B])
        eqo = sb("eqo", [P, 4, B])
        trow = sb("trow", [1, 2 * P])
        rtok = sb("rtok", [P, B * NT])
        vaug_f = vaug[:, :, :, :, :].rearrange("p a k h c -> p (a k h c)").rearrange("p (n t) -> p n t", t=S)
        act_s, u_s, h_s, yT = vaug_f[:, 0:2], vaug_f[:, 2:4], vaug_f[:, 4:7], vaug_f[:, 7]
        y_s = sb("y_s", [P, 2, NT, P])

        def tiles(flat, first, count):
            return [flat[:, S * k:S * k + S] for k in range(first, first + count)]

        qst_f = qst[:, :, :, :].rearrange("p a h t -> p (a h t)").bitcast(F32)
        early_u = (tiles(y_s[:, :, :, :].rearrange("p a i d -> p (a i d)"), 0, 2) + [yT]
                   + tiles(pt_f, 2, 2 * PT - 2)
                   + tiles(rope[:, :, :, :].rearrange("p a c t -> p (a c t)"), 0, 6)
                   + tiles(xin[:, :, :, :].rearrange("p b i d -> p (b i d)"), 0, B)
                   + tiles(qst_f, 4, 4) + tiles(kst_f.bitcast(F32), 7, 1)
                   + tiles(parts[:, :, :, :].rearrange("p a c t -> p (a c t)").bitcast(F32), 0, 3)
                   + [cosT, sinT] + tiles(osb[:, :, :].rearrange("p a t -> p (a t)"), 0, 2)
                   + [t[:, :, :].rearrange("p i d -> p (i d)") for t in (xn, ot, otT, xbo)]
                   + [xnT[:, :], ctT[:, :], wa_s[:, 0:S]] + tiles(selc_s[:, :], 0, 2))

        bank = [ctx.enter_context(nc.psum_tensor(f"bank{i}", [P, 512], F32)) for i in range(2)]
        stp = ctx.enter_context(nc.psum_tensor("stp", [P, 2, 2, S], F32))
        obank = ctx.enter_context(nc.psum_tensor("obank", [P, S], F32))
        misc = ctx.enter_context(nc.psum_tensor("misc", [P, 512], F32))

        loaded_w = sem("loaded_w")
        loaded_x = [sem(f"loaded_x{b}") for b in range(B)]
        loaded_ffn = sem("loaded_ffn")
        consts_ready = sem("consts_ready")
        vzero = sem("vzero")
        misc_filled = sem("misc_filled")
        misc_free = sem("misc_free")
        xn_ready = sem("xn_ready")
        var_ready = sem("var_ready")
        rstd_ready = sem("rstd_ready")
        parts_ready = sem("parts_ready")
        parts_stored = [sem(f"parts_stored{b}") for b in range(B)]
        stacks_ready = [sem(f"stacks_ready{i}") for i in range(2)]
        nat_filled = sem("nat_filled")
        nat_free = sem("nat_free")
        mparts_ready = sem("mparts_ready")
        mrows_ready = [sem(f"mrows_ready{i}") for i in range(2)]
        st_filled = sem("st_filled")
        exp_done = sem("exp_done")
        pv_done = sem("pv_done")
        o_out = sem("o_out")
        xbo_ready = sem("xbo_ready")
        xn2_ready = sem("xn2_ready")
        logits_ready = sem("logits_ready")
        rexp_ready = sem("rexp_ready")
        sc_ready = sem("sc_ready")
        swap_in = sem("swap_in")
        swapped = sem("swapped")
        rmat_in = sem("rmat_in")
        rmat_out = sem("rmat_out")
        fsp_ready = sem("fsp_ready")
        fs_ready = sem("fs_ready")
        gate_out = sem("gate_out")
        early_done = sem("early_done")
        den_done = sem("den_done")
        up_filled = sem("up_filled")
        gate_filled = sem("gate_filled")
        mask_filled = sem("mask_filled")
        silu_done = sem("silu_done")
        u_done = sem("u_done")
        h_done = sem("h_done")
        down_done = sem("down_done")
        yT_ready = sem("yT_ready")
        yt_filled = sem("yt_filled")
        y_ready = sem("y_ready")
        stored = [sem("stored0"), sem("stored1")]
        dve_step = sem("dve_step")
        pool_step = sem("pool_step")

        def pre_bank(b, k):
            if b:
                return misc[:, :]
            return (misc[:, :], bank[0][:, :], bank[1][:, :], stp[:, 0, 0], stp[:, 0, 1], stp[:, 1, 0],
                    stp[:, 1, 1], obank[:, :], misc[:, :])[k]

        block = ctx.enter_context(nc.Block())

        def h2(q, g1):
            return 4 * (q // 2) + 2 * g1 + q % 2

        @block.sync
        def _(sp):
            sp.dma_start(xin[:, 0], x[0].rearrange("(p i) d -> p i d", i=NT)).then_inc(loaded_x[0], 16)
            for dst, src in ((trig_s[:, KCOS:], trig[:, KCOS:]), (rows_s[:, :], rows[0].partition_broadcast(P))):
                sp.dma_start(dst, src).then_inc(loaded_w, 16)
            for b in range(1, B):
                sp.dma_start(xin[:, b], x[b].rearrange("(p i) d -> p i d", i=NT)).then_inc(loaded_x[b], 16)
            for dst, src in ((wup_s[:, :], wup), (wgate_s[:, :], wgate),
                             (wdown_s[:, :, :], wdown.rearrange("p (n d) -> p n d", n=NE)),
                             (bdown_s[:, :], bdown), (selc_s[0:96, :], selc), (cst_s[:, :], cst),
                             (kdig_s[:, :, :], kdig.rearrange("p (s k) -> p s k", k=16))):
                sp.dma_start(dst, src).then_inc(loaded_ffn, 16)

            def stack(b):
                for a in range(2):
                    sp.wait_ge(parts_ready, 2 * b + a + 1)
                    for hp in range(2):
                        sp.dma_start(parts_dram[b, a, hp].rearrange("(c d) (h t) -> (d h) c t", c=3, h=8),
                                     parts[64 * hp:64 * hp + 64, a]).then_inc(parts_stored[b], 16)
                    sp.wait_ge(parts_stored[b], 32 * (a + 1))
                    if b < 2:
                        sp.wait_ge(vzero, 1)
                    if b >= 2 and a == 0:
                        sp.wait_ge(st_filled, 32 * (b - 1))
                    for hp in range(2):
                        for r0, reps in ((0, 3), (24, 2), (40, 1)):
                            r = 64 * hp + r0
                            if a == 0:
                                sp.dma_start(qst[r:r + 8 * reps, b % 2],
                                             parts_dram[b, 0, hp, 0:8 * reps].rearrange("r (h t) -> r h t", h=8))\
                                  .then_inc(stacks_ready[b % 2], 16)
                            else:
                                part = 3 - reps
                                src = parts_dram[b, 1, hp, 8 * part:8 * part + 8]
                                sp.dma_start(kst[r:r + 8 * reps, b % 2],
                                             src.unsqueeze(0).broadcast_to([reps, 8, 8 * S]))\
                                  .then_inc(stacks_ready[b % 2], 16)

            def mrows(g):
                b, q = divmod(g, NQ)
                sp.wait_ge(nat_free, mt_use(g) + 1)
                for p in range(MROWS):
                    for hp in range(2):
                        a = h2(q, 0)
                        r, m = 64 * hp + QROWS + p, 4 * p + 2 * hp
                        sp.dma_start(qst[r:r + 1, b % 2, a:a + 3:2, :], mts[m:m + 2, g % 2, :])\
                          .then_inc(mrows_ready[g % 2], 16)

            stack(0)
            for b in range(B):
                for q in range(NQ):
                    if q == 2 and b + 1 < B:
                        stack(b + 1)
                    mrows(NQ * b + q)
            sp.wait_ge(swap_in, 1)
            for k in range(2):
                sp.dma_start(other[64 * k:64 * k + 64, :], ping[0][64 - 64 * k:128 - 64 * k, :]).then_inc(swapped, 16)
            sp.wait_ge(fsp_ready, 1)
            for half in range(2):
                tok = msf.rearrange("e (b h t) -> e b h t", b=B, h=2)[:, :, half]
                sp.dma_start(tok, ping[0][64 * half:64 * half + 64, :].rearrange("e (b t) -> e b t", b=B))\
                  .then_inc(fs_ready, 16)
            for part in range(3):
                if part:
                    sp.wait_ge(fsp_ready, 1 + part)
                for half in range(2):
                    for eg in range(2):
                        r = 64 * half + 32 * eg
                        tok = fs[32 * part:32 * part + 32, eg].rearrange("e (b h t) -> e b h t", b=B, h=2)[:, :, half]
                        sp.dma_start(tok, fsp[r:r + 32, part].rearrange("e (b t) -> e b t", b=B)).then_inc(fs_ready, 16)
            for blk in range(B):
                sp.wait_ge(y_ready, blk + 1)
                sp.dma_start(out[blk].rearrange("(p i) d -> p i d", i=NT), y_s[:, blk % 2])\
                  .then_inc(stored[blk % 2], 16)
            for k in range(2):
                sp.wait_ge(stored[k], 16 * B // 2)

        @block.gpsimd
        def _(pool):
            steps = [0]

            def link(ins):
                steps[0] += 1
                ins.then_inc(pool_step, 1)
                pool.wait_ge(pool_step, steps[0])

            def rsqrt(k):
                pool.wait_ge(var_ready, k + 1)
                pool.tensor_tensor(rstd[:, :], vare[:, :], half_neg[:, :], ALU.pow).then_inc(rstd_ready, 1)

            link(pool.memset(half_neg[:, :], -0.5))
            rsqrt(0)
            pool.wait_ge(loaded_w, 96)
            pool.tensor_copy(identb[:, :], ident).then_inc(consts_ready, 1)
            pool.memset(vaug[:, :, :, :, :], 0.0).then_inc(pool_step, 1)
            steps[0] += 1
            pool.memset(kst[:, :, :, :], 1.0).then_inc(vzero, 1)
            pool.wait_ge(pool_step, steps[0])
            v = vaug[:, :, :, :, :].rearrange("p a k (f j) c -> p (a k f) j c", j=2)
            for j in range(2):
                pool.memset(v[:, :, j, 16 * j + 8:16 * j + 9], 1.0).then_inc(vzero, 1)

            def split(b):
                for a in range(2):
                    pool.wait_ge(misc_free, pre_base(b) + 5 + 3 * a)
                    link(pool.tensor_tensor(rope[:, a, 2], rope[:, a, 2], rope[:, a, 1], ALU.add))
                    pool.wait_ge(parts_stored[b - 1], 64)
                    link(pool.tensor_copy(parts[:, a, 0], rope[:, a, 2]))
                    link(pool.tensor_tensor(rope[:, a, 1], rope[:, a, 2], parts[:, a, 0], ALU.subtract))
                    link(pool.tensor_copy(parts[:, a, 1], rope[:, a, 1]))
                    pool.tensor_tensor(parts[:, a, 2], rope[:, a, 1], parts[:, a, 1], ALU.subtract)\
                        .then_inc(parts_ready, 1)

            def residual(b):
                pool.wait_ge(loaded_x[b], 16)
                if b:
                    pool.wait_ge(misc_free, post_base(b - 1) + 4)
                pool.tensor_tensor(xbo[:, :, :], xin[:, b],
                                   rows_s[:, 128:256].unsqueeze(1).broadcast_to([P, NT, P]), ALU.add)\
                    .then_inc(xbo_ready, 1)

            k = 1
            for b in range(B + 2):
                if b < B:
                    if b:
                        rsqrt(k)
                        k += 1
                        split(b)
                if b == 0:
                    residual(0)
                if 2 <= b:
                    rsqrt(k)
                    k += 1
                    if b - 1 < B:
                        residual(b - 1)
            pool.wait_ge(loaded_ffn, 112)
            pool.tensor_copy(sel_s[:, :], selc_s[0:96, :]).then_inc(consts_ready, 1)
            pool.wait_ge(pv_done, NT * NQUAD)
            pool.wait_ge(parts_stored[B - 1], 64)
            pool.wait_ge(misc_free, post_base(B - 1) + NPOST)
            for t in range(EARLY):
                pool.wait_ge(silu_done, t + 1)
                pool.wait_ge(gate_out, t + 1)
                pool.tensor_tensor(early_u[t], act_s[:, t % 2], u_s[:, t % 2], ALU.mult).then_inc(early_done, 1)

        @block.scalar
        def _(act):
            def pre_task(b, k):
                base = pre_base(b) + k + 1
                if k == 0:
                    act.wait_ge(misc_filled, base)
                    if b:
                        act.wait_ge(misc_free, base - 1)
                    nc.scalar.activation(xnT[:, :].rearrange("d (p i) -> d i p", i=NT),
                                         pre_bank(b, k).rearrange("d (i p) -> d i p", i=NT), ACT.Copy)\
                        .then_inc(misc_free, 1)
                if k == 1:
                    act.wait_ge(misc_filled, base)
                    nc.scalar.activation(ctT[:, :], pre_bank(b, k), ACT.Identity, bias=cols_s[:, CBD:CBD + 1])\
                        .then_inc(misc_free, 1)

            def post_task(b, k):
                base = post_base(b) + k + 1
                if k == 2:
                    act.wait_ge(misc_filled, base)
                    nc.scalar.activation(otT[:, :, :], misc[:, :], ACT.Copy).then_inc(misc_free, 1)
                if k == 4:
                    act.wait_ge(misc_filled, base)
                    nc.scalar.activation(x2T[:, S * b:S * b + S].rearrange("d (p i) -> d i p", i=NT),
                                         misc[:, :].rearrange("d (i p) -> d i p", i=NT), ACT.Copy)\
                        .then_inc(misc_free, 1)
                if k == 6:
                    act.wait_ge(misc_filled, base)
                    nc.scalar.activation(scT[:, RUN * b:RUN * b + RUN], misc[:, 0:RUN], ACT.Copy)\
                        .then_inc(misc_free, 1)

            def router_exp(b):
                act.wait_ge(logits_ready, b + 1)
                nc.scalar.activation(sc[:, :, :], sc[:, :, :], ACT.Exp).then_inc(rexp_ready, 1)

            def ffn_out(blk):
                act.wait_ge(down_done, NE * (blk + 1))
                if blk:
                    act.wait_ge(yt_filled, blk)
                nc.scalar.activation(yT, obank[:, :], ACT.Copy).then_inc(yT_ready, 1)

            for dst, src in ((trig_s[:, 0:KCOS], trig[:, 0:KCOS]), (wa_s[:, :], wa), (cols_s[:, :], cols), (wb_s[:, :], wb)):
                act.dma_start(dst, src).then_inc(loaded_w, 16)
            act.wait_ge(loaded_w, 96)
            for k in range(2):
                pre_task(0, k)
            for n in range(SLOTS + 64):
                u = (n - ST_LAG) // 2
                if (n - ST_LAG) % 2 == 0 and 0 <= u < UQ * NQUAD:
                    act.wait_ge(st_filled, u + 1)
                    if u >= PT:
                        act.wait_ge(pv_done, (u - PT) // 2 + 1)
                    nc.scalar.activation(pt[:, u % PT], stp[:, u % 2], ACT.Exp, scale=SCALE)\
                        .then_inc(exp_done, 1)
                if (n - ST_LAG) % 2 == 0 and u % UQ == 2 and (u // UQ) % 2 == 0 and 0 < u // UQ <= NQUAD:
                    g = u // UQ - 1
                    s = (g % NQ) // 2
                    act.wait_ge(pv_done, NT * (g + 1))
                    if g >= NQ:
                        act.wait_ge(misc_filled, post_base(g // NQ - 1) + s + 1)
                    nc.scalar.activation(osb[:, s], obank[:, :], ACT.Copy).then_inc(o_out, 1)
                for b in range(1, B):
                    for k in range(2):
                        if n == pre_slot(b, k):
                            pre_task(b, k)
                for b in range(B):
                    for k in (2, 4, 6):
                        if n == post_slot(b, k):
                            post_task(b, k)
                    if n == post_slot(b, 5) + 2:
                        router_exp(b)
            act.wait_ge(loaded_ffn, 112)
            act.wait_ge(pv_done, NT * NQUAD)
            for t in range(B * NE):
                n = t % NE
                act.wait_ge(up_filled, t + 1)
                if t >= 2:
                    act.wait_ge(early_done, min(t - 1, EARLY))
                if t >= EARLY + 2:
                    act.wait_ge(u_done, t - 1 - EARLY)
                nc.scalar.activation(act_s[:, t % 2], bank[t % 2][:, :], ACT.Silu,
                                     bias=cols_s[:, CUP + n:CUP + n + 1]).then_inc(silu_done, 1)
                if t < EARLY:
                    act.wait_ge(gate_filled, t + 1)
                    nc.scalar.activation(u_s[:, t % 2], stp[:, 0, t % 2], ACT.Identity,
                                         bias=cols_s[:, CGT + n:CGT + n + 1]).then_inc(gate_out, 1)
                if t == EARLY - 1:
                    for blk in range(EARLY // NE - 1):
                        ffn_out(blk)
                if t % NE == 1 and t > EARLY:
                    ffn_out(t // NE - 1)
            ffn_out(B - 1)

        @block.tensor
        def _(pe):
            def tile_w(c):
                return wa_s[:, c:c + P]

            def pre_task(b, k):
                base = pre_base(b) + k
                if b:
                    pe.wait_ge(misc_free, base)
                elif k:
                    pe.wait_ge(misc_free, min(k, 2))
                if k == 0:
                    pe.wait_ge(xn_ready, b + 1)
                    for i in range(NT):
                        last = nc.tensor.transpose(pre_bank(b, k)[:, P * i:P * i + P], xn[:, i], ident)
                elif k == 1:
                    last = nc.tensor.matmul(pre_bank(b, k), tile_w(WD), xnT[:, :], start=True, stop=True)
                elif k in (2, 3, 4):
                    c = (WQR, WQRS, WUQ)[k - 2]
                    last = nc.tensor.matmul(pre_bank(b, k), wb_s[0:64, c:c + P], ctT[0:64, :], start=True, stop=True)
                elif k in (5, 6):
                    last = nc.tensor.matmul(pre_bank(b, k), tile_w((WKR, WKRS)[k - 5]), xnT[:, :], start=True, stop=True)
                elif k == 7:
                    last = nc.tensor.matmul(pre_bank(b, k), wb_s[64:128, WUK:WUK + P], ctT[64:128, :],
                                            start=True, stop=True)
                else:
                    for i in range(NT):
                        last = nc.tensor.matmul(pre_bank(b, k)[:, P * i:P * i + P], ctT[64:128, P * i:P * i + P],
                                                wb_s[64:128, WUV:WUV + P], start=True, stop=True)
                last.then_inc(misc_filled, 1)

            def post_task(b, k):
                pe.wait_ge(misc_free, post_base(b) + k)
                if k in (0, 1):
                    pe.wait_ge(o_out, 2 * b + k + 1)
                    for i in range(NT):
                        last = nc.tensor.transpose(misc[:, P * i:P * i + P], osb[:, k, i::NT], ident)
                elif k == 2:
                    for i in range(NT):
                        last = nc.tensor.transpose(misc[:, P * i:P * i + P], ot[:, i], ident)
                elif k == 3:
                    for i in range(NT):
                        last = nc.tensor.matmul(misc[:, P * i:P * i + P], otT[:, i], tile_w(WO), start=True, stop=True)
                elif k == 4:
                    pe.wait_ge(xn2_ready, b + 1)
                    for i in range(NT):
                        last = nc.tensor.transpose(misc[:, P * i:P * i + P], xn[:, i], ident)
                elif k == 5:
                    for i in range(NT):
                        c = S * b + P * i
                        last = nc.tensor.matmul(misc[:, E * i:E * i + E], x2T[:, c:c + P], wa_s[:, WR:WR + E],
                                                start=True, stop=True)
                else:
                    pe.wait_ge(sc_ready, b + 1)
                    for i in range(NT):
                        r, c = 64 * (i // 2), P * (i % 2)
                        last = nc.tensor.matmul(misc[r:r + 64, c:c + P], sc[:, i], ident, start=True, stop=True)
                last.then_inc(misc_filled, 1)

            def nat(n):
                g, i = divmod(n, 16)
                b, q = divmod(g, NQ)
                t, g1, hp = i // 4, i // 2 % 2, i % 2
                if i == 0 and q == 0:
                    pe.wait_ge(stacks_ready[b % 2], 16 * 12 * (b // 2 + 1))
                use = nat_use(n)
                if use >= 2:
                    pe.wait_ge(nat_free, use - 1)
                r, h = 64 * hp, h2(q, g1)
                nc.tensor.matmul(bank[use % 2][:, :], qst[r:r + QROWS, b % 2, h, P * t:P * t + P],
                                 kst[r:r + QROWS, b % 2, h, :], start=True, stop=True).then_inc(nat_filled, 1)

            def max_rows(g):
                use = mt_use(g)
                pe.wait_ge(nat_free, use - 1)
                pe.wait_ge(mparts_ready, g + 1)
                o = bank[use % 2][0:4 * MROWS, 0:S // 2].bitcast(BF16)
                for t in range(NT):
                    last = nc.tensor.transpose(o[:, P * t:P * t + P],
                                               mpart[:, g % 2, t].rearrange("p a b -> p (a b)"), identb[:, :])
                last.then_inc(nat_filled, 1)

            def scores(u):
                g, k = divmod(u, UQ)
                b, q = divmod(g, NQ)
                kt, g1 = divmod(k, 2)
                if k == 0:
                    pe.wait_ge(mrows_ready[g % 2], 16 * 2 * MROWS * (g // 2 + 1))
                if u >= 2:
                    pe.wait_ge(exp_done, u - 1)
                h = h2(q, g1)
                for hp in range(2):
                    r = 64 * hp
                    last = nc.tensor.matmul(stp[:, u % 2, hp], kst[r:r + KST, b % 2, h, P * kt:P * kt + P],
                                            qst[r:r + KST, b % 2, h, :], start=True, stop=True)
                last.then_inc(st_filled, 1)

            def weigh(v):
                g, kt = divmod(v, NT)
                b, q = divmod(g, NQ)
                j = q % 2
                pe.wait_ge(exp_done, 2 * v + 2)
                if kt == 0:
                    pe.wait_ge(misc_free, pre_base(b) + NPRE)
                if kt == 0 and j == 0 and g:
                    pe.wait_ge(o_out, g // 2)
                for hp in range(2):
                    for g1 in range(2):
                        c = 32 * (2 * hp + g1)
                        last = nc.tensor.matmul(obank[c:c + 32, :], vaug[:, b % 2, kt, 8 * hp + h2(q, g1)],
                                                pt[:, (2 * v + g1) % PT, hp], start=(j == 0 and kt == 0),
                                                stop=(j == 1 and kt == NT - 1), tile_position=(0, c))
                last.then_inc(pv_done, 1)

            def up_gate(t):
                blk, n = divmod(t, NE)
                xb = x2T[:, S * blk:S * blk + S]
                if t >= 2:
                    pe.wait_ge(silu_done, t - 1)
                nc.tensor.matmul(bank[t % 2][:, :], wup_s[:, P * n:P * n + P], xb, start=True, stop=True)\
                    .then_inc(up_filled, 1)
                if t >= 2:
                    pe.wait_ge(gate_out, min(t - 1, EARLY))
                if t >= EARLY + 2:
                    pe.wait_ge(u_done, t - 1 - EARLY)
                nc.tensor.matmul(stp[:, 0, t % 2], wgate_s[:, P * n:P * n + P], xb, start=True, stop=True)\
                    .then_inc(gate_filled, 1)

            pe.wait_ge(loaded_w, 96)
            for k in range(NPRE):
                pre_task(0, k)
            pe.wait_ge(consts_ready, 1)
            pe.wait_ge(vzero, 3)
            used = [NPRE, 0]

            def keep_clock(n):
                if n - used[1] >= 3 and n < 16 * NQUAD:
                    pe.wait_ge(misc_free, used[0])
                    nc.tensor.matmul(misc[:, :], identb[:, :], identb[:, :].unsqueeze(1).broadcast_to([P, NT, P]),
                                     start=True, stop=True)

            for n in range(SLOTS + 64):
                keep_clock(n)
                if n < 16 * NQUAD:
                    nat(n)
                if n >= 16 and n % 16 == 3 and n // 16 <= NQUAD:
                    max_rows(n // 16 - 1)
                if (n - ST_LAG) % 2 == 0 and n >= ST_LAG:
                    u = (n - ST_LAG) // 2
                    if u < UQ * NQUAD:
                        scores(u)
                    if u >= PV_LAG and (u - PV_LAG) % 2 == 0 and u - PV_LAG < UQ * NQUAD:
                        weigh((u - PV_LAG) // 2)
                for b in range(1, B):
                    for k in range(NPRE):
                        if n == pre_slot(b, k):
                            pre_task(b, k)
                            used[:] = used[0] + 1, n
                for b in range(B):
                    for k in range(NPOST):
                        if n == post_slot(b, k):
                            if b == B - 1 and k in (4, 6):
                                if k == 4:
                                    pe.wait_ge(loaded_ffn, 112)
                                    pe.wait_ge(nat_free, mt_use(NQUAD - 1) + 1)
                                up_gate(k // 2 - 2)
                            post_task(b, k)
                            used[:] = used[0] + 1, n

            for t in range(2, EARLY_FIRST):
                up_gate(t)

            def summed(k, jobs):
                pe.wait_ge(rmat_in, k + 1)
                for c, w, mat, rhs in jobs:
                    last = nc.tensor.matmul(misc[:, c:c + w], cst_s[:, mat:mat + P], rhs, start=True, stop=True)
                last.then_inc(rmat_out, 1)

            for s in range(DIGITS):
                summed(s, [(0, 16, KONE, cnt[:, :])])
                for k in range(EARLY_DIGIT):
                    up_gate(EARLY_FIRST + s * EARLY_DIGIT + k)
            done = EARLY_FIRST + DIGITS * EARLY_DIGIT
            summed(DIGITS, [(0, 1, KONE, one[:, 0:1]), (1, NB, KTRI, eq[:, :]), (17, NB, KBLK, eq[:, :]),
                            (33, 1, KBELOW, one[:, 1:2])])
            pe.wait_ge(rmat_in, DIGITS + 2)
            nc.tensor.transpose(misc[0:1, 0:P], one[:, 4:5], ident).then_inc(rmat_out, 1)
            pe.wait_ge(rmat_in, DIGITS + 3)
            nc.tensor.transpose(misc[:, P:P + 1], trow[0:1, P:2 * P], ident[0:1, 0:1]).then_inc(rmat_out, 1)
            for k in range(EARLY_COUNT):
                up_gate(done + k)
            summed(DIGITS + 3, [(0, 2, KPAIR, one[:, 6:8]), (2, B, KOTHER, eqc[:, :]), (2 + B, B, KNEXT, eqc[:, :])])
            for t in range(done + EARLY_COUNT, EARLY):
                up_gate(t)
            pe.wait_ge(fsp_ready, 3)
            for k in range(B * NT):
                b, i = divmod(k, NT)
                for half in range(2):
                    r = 64 * half
                    last = nc.tensor.matmul(misc[r:r + 64, k:k + 1], ping[0][:, RUN * b + i:RUN * b + RUN:NT],
                                            cst_s[:, KBLK + r:KBLK + r + 1], start=True, stop=True)
            last.then_inc(den_done, 1)

            pe.wait_ge(loaded_ffn, 112)
            pe.wait_ge(consts_ready, 2)
            pe.wait_ge(gate_out, EARLY)

            def mask(t):
                blk, n = divmod(t, NE)
                if t >= 2:
                    pe.wait_ge(h_done, t - 1)
                if t == DIRECT:
                    pe.wait_ge(fs_ready, 16 * 14)
                if t < DIRECT:
                    for half in range(2):
                        r = 64 * half
                        for part in range(3):
                            last = nc.tensor.matmul(stp[:, 1 - half, t % 2, 0:RUN], sel_s[r:r + 32, P * n:P * n + P],
                                                    fsp[r:r + 32, part, RUN * blk:RUN * blk + RUN],
                                                    start=part == 0, stop=part == 2)
                else:
                    last = nc.tensor.matmul(stp[:, 1, t % 2], sel_s[:, P * (n % 8):P * (n % 8) + P],
                                            fs[:, n // 8, S * blk:S * blk + S], start=True, stop=True)
                last.then_inc(mask_filled, 1)

            def down(t):
                blk, n = divmod(t, NE)
                pe.wait_ge(h_done, t + 1)
                if n == 0 and blk:
                    pe.wait_ge(yT_ready, blk)
                if n == NE - 1:
                    nc.tensor.matmul(obank[:, :], bdown_s[:, :], msf[:, S * blk:S * blk + S], start=False, stop=False)
                nc.tensor.matmul(obank[:, :], wdown_s[:, n], h_s[:, t % 3], start=n == 0, stop=n == NE - 1)\
                    .then_inc(down_done, 1)

            def back(blk):
                pe.wait_ge(yT_ready, blk + 1)
                if blk:
                    pe.wait_ge(y_ready, blk)
                for i in range(NT):
                    last = nc.tensor.transpose(misc[:, P * i:P * i + P], vaug_f[:, 7, i::NT], ident)
                last.then_inc(yt_filled, 1)

            for t in range(B * NE):
                blk, n = divmod(t, NE)
                if t >= EARLY:
                    up_gate(t)
                mask(t)
                if t >= 2:
                    down(t - 2)
                if n == 5 and blk:
                    back(blk - 1)
            down(B * NE - 2)
            down(B * NE - 1)
            back(B - 1)

        @block.vector
        def _(dve):
            steps = [0]
            V = nc.vector

            def link(ins):
                steps[0] += 1
                ins.then_inc(dve_step, 1)
                dve.wait_ge(dve_step, steps[0])

            def norm_stats(src):
                for i in range(NT):
                    last = V.bn_stats(stats[:, i], src[:, i])
                link(last)
                for i in range(NT):
                    last = V.bn_aggr(mv[:, i], stats[:, i])
                link(last)
                V.tensor_scalar(vare[:, :], mv[:, :, 1], EPS, None, ALU.add).then_inc(var_ready, 1)

            def norm_apply(src, k):
                dve.wait_ge(rstd_ready, k + 1)
                for i in range(NT):
                    last = V.tensor_scalar(xn[:, i], src[:, i], mv[:, i, 0:1], rstd[:, i:i + 1],
                                           ALU.subtract, ALU.mult)
                return last

            first_norm, second_norm = (0, 1, 2, 4), (3, 5, 6, 7)

            def pre_stats(b):
                dve.wait_ge(loaded_x[b], 16)
                norm_stats(xin[:, b])

            def pre_norm(b):
                norm_apply(xin[:, b], first_norm[b]).then_inc(xn_ready, 1)

            def pre_task(b, k):
                dve.wait_ge(misc_filled, pre_base(b) + k + 1)
                if k in (2, 3, 5, 6):
                    a, c = divmod(k - 2, 3)
                    if b:
                        dve.wait_ge(parts_ready, 2 * (b - 1) + a + 1)
                    col = ((CAQ, CBQ), (CAK, CBK))[a][c]
                    V.scalar_tensor_tensor(out=rope[:, a, c], in0=pre_bank(b, k), scalar=cols_s[:, col:col + 1],
                                           in1=(cosT, sinT)[c], op0=ALU.add, op1=ALU.mult).then_inc(misc_free, 1)
                elif k in (4, 7):
                    a = (k - 4) // 3
                    col = (CCQ, CCK)[a]
                    dve.wait_ge(misc_free, pre_base(b) + k)
                    V.scalar_tensor_tensor(out=rope[:, a, 2], in0=pre_bank(b, k), scalar=cols_s[:, col:col + 1],
                                           in1=rope[:, a, 0], op0=ALU.add, op1=ALU.add).then_inc(misc_free, 1)
                elif k == 8:
                    dve.wait_ge(vzero, 3)
                    if b >= 2:
                        dve.wait_ge(pv_done, NT * NQ * (b - 1))
                    m = pre_bank(b, k).rearrange("p (k f j d) -> p (k f) j d", k=NT, j=2, d=HD)
                    bv = rows_s[:, 0:128].rearrange("p (f j d) -> p f j d", j=2, d=HD)
                    vv = vaug[:, b % 2].rearrange("p k (f j) c -> p k f j c", j=2)
                    mm = pre_bank(b, k).rearrange("p (k f j d) -> p k f j d", k=NT, j=2, d=HD)
                    for j in range(2):
                        last = V.tensor_tensor(vv[:, :, :, j, 16 * j:16 * j + HD], mm[:, :, :, j, :],
                                               bv[:, :, j, :].unsqueeze(1).broadcast_to([P, NT, H // 2, HD]), ALU.add)
                        if j == 0:
                            link(last)
                    last.then_inc(misc_free, 1)

            def split_first(a):
                link(V.tensor_tensor(rope[:, a, 2], rope[:, a, 2], rope[:, a, 1], ALU.add))
                link(V.tensor_copy(parts[:, a, 0], rope[:, a, 2]))
                link(V.tensor_tensor(rope[:, a, 1], rope[:, a, 2], parts[:, a, 0], ALU.subtract))
                link(V.tensor_copy(parts[:, a, 1], rope[:, a, 1]))
                V.tensor_tensor(parts[:, a, 2], rope[:, a, 1], parts[:, a, 1], ALU.subtract).then_inc(parts_ready, 1)

            def post_task(b, k):
                if k in (0, 1, 3, 5):
                    dve.wait_ge(misc_filled, post_base(b) + k + 1)
                if k in (0, 1):
                    m = misc[:, :].rearrange("p (r c) -> p r c", c=16)
                    link(V.reciprocal(rden[:, k], m[:, :, 8]))
                    V.tensor_tensor(ot[:, :, 64 * k:64 * k + 64].rearrange("p i (r d) -> p i r d", d=HD),
                                    misc[:, :].rearrange("p (i r c) -> p i r c", i=NT, c=16)[:, :, :, 0:HD],
                                    rden[:, k].rearrange("p (i r) -> p i r", i=NT)
                                    .unsqueeze(3).broadcast_to([P, NT, 8, HD]), ALU.mult).then_inc(misc_free, 1)
                elif k == 3:
                    dve.wait_ge(xbo_ready, b + 1)
                    V.tensor_tensor(x2[:, b], misc[:, :].rearrange("p (i d) -> p i d", d=P), xbo[:, :, :], ALU.add)\
                        .then_inc(misc_free, 1)
                    dve.wait_ge(misc_free, post_base(b) + k + 1)
                    norm_stats(x2[:, b])
                elif k == 5:
                    V.tensor_tensor(sc[:, :, :], misc[:, 0:NT * E].rearrange("p (i e) -> p i e", e=E),
                                    rows_s[:, 256:320].unsqueeze(1).broadcast_to([P, NT, E]), ALU.add)\
                        .then_inc(misc_free, 1)
                    dve.wait_ge(misc_free, post_base(b) + k + 1)
                    link(V.tensor_reduce(srow[:, 0], sc[:, :, :], AX, ALU.max))
                    V.tensor_tensor(sc[:, :, :], sc[:, :, :], srow[:, 0].unsqueeze(2).broadcast_to([P, NT, E]),
                                    ALU.subtract).then_inc(logits_ready, 1)

            def router_norm(b):
                dve.wait_ge(rexp_ready, b + 1)
                link(V.tensor_reduce(srow[:, 1], sc[:, :, :], AX, ALU.add))
                link(V.reciprocal(srow[:, 2], srow[:, 1]))
                V.tensor_tensor(sc[:, :, :], sc[:, :, :], srow[:, 2].unsqueeze(2).broadcast_to([P, NT, E]),
                                ALU.mult).then_inc(sc_ready, 1)

            def row_max(n):
                g, i = divmod(n, 16)
                t, c = i // 4, 2 * (i % 2) + i // 2 % 2
                use = nat_use(n)
                dve.wait_ge(nat_filled, use + 1)
                V.tensor_reduce(mx[:, g % 2, t, c:c + 1], bank[use % 2][:, :], AX, ALU.max).then_inc(nat_free, 1)

            def max_parts(g):
                dve.wait_ge(nat_free, nat_use(16 * g + 15) + 1)
                if g >= 2:
                    dve.wait_ge(nat_filled, mt_use(g - 2) + 1)
                m = mx[:, g % 2]
                link(V.tensor_scalar(mpart[:, g % 2, :, 0], m, -1.0, None, ALU.mult))
                V.scalar_tensor_tensor(out=mpart[:, g % 2, :, 1], in0=m, scalar=-1.0, in1=mpart[:, g % 2, :, 0],
                                       op0=ALU.mult, op1=ALU.subtract).then_inc(mparts_ready, 1)

            def max_rows(g):
                use = mt_use(g)
                dve.wait_ge(nat_filled, use + 1)
                if g >= 2:
                    dve.wait_ge(mrows_ready[g % 2], 32 * MROWS * (g // 2))
                V.tensor_copy(mts[:, g % 2, :], bank[use % 2][0:4 * MROWS, 0:S // 2].bitcast(BF16))\
                    .then_inc(nat_free, 1)

            def exchange(top_d, low_d, top_s, low_s):
                V.tensor_tensor(top_d, top_s, low_s, ALU.max)
                link(V.tensor_tensor(low_d, top_s, low_s, ALU.min))

            def sort_stage(k, c0, c1):
                m, d = SORT[k]
                src, dst = (scT if k == 0 else ping[(k - 1) % 2])[:, c0:c1], ping[k % 2][:, c0:c1]
                if d == 0:
                    s_, d_ = (t.rearrange("p (n m) -> p n m", m=m) for t in (src, dst))
                    stop = m // 2 - 1 if m > 2 else 0
                    if m == 2:
                        exchange(d_[:, :, 0:1], d_[:, :, 1:2], s_[:, :, 0:1], s_[:, :, 1:2])
                    else:
                        exchange(d_[:, :, 0:m // 2], d_[:, :, m - 1:stop:-1], s_[:, :, 0:m // 2], s_[:, :, m - 1:stop:-1])
                else:
                    s_, d_ = (t.rearrange("p (n a k) -> p n a k", a=2, k=d) for t in (src, dst))
                    exchange(d_[:, :, 0], d_[:, :, 1], s_[:, :, 0], s_[:, :, 1])

            def sort_b(b, ks):
                dve.wait_ge(misc_free, post_base(b) + NPOST)
                for k in ks:
                    sort_stage(k, RUN * b, RUN * b + RUN)

            def merge(b2, ks):
                for k in ks:
                    sort_stage(k, S * (b2 - 1), S * b2)

            pre_stats(0)
            pre_norm(0)
            dve.wait_ge(loaded_w, 96)
            for k in range(2, NPRE):
                pre_task(0, k)
                if k in (4, 7):
                    dve.wait_ge(misc_free, k + 1)
                    split_first(k // 7)
            for n in range(SLOTS + 64):
                for b in range(1, B):
                    if n == pre_slot(b, 0) - 4:
                        pre_stats(b)
                    if n == pre_slot(b, 0) - 2:
                        pre_norm(b)
                    for k in range(2, NPRE):
                        if n == pre_slot(b, k) + 1:
                            pre_task(b, k)
                for b in range(B):
                    for k in range(NPOST):
                        if n == post_slot(b, k) + 1:
                            post_task(b, k)
                    if n == post_slot(b, 3) + 3:
                        norm_apply(x2[:, b], second_norm[b]).then_inc(xn2_ready, 1)
                    if n == post_slot(b, 5) + 4:
                        router_norm(b)
                if n < 16 * NQUAD:
                    row_max(n)
                if n % 16 == 15 and n // 16 < NQUAD:
                    max_parts(n // 16)
                if n >= 16 and n % 16 == 3 and n // 16 <= NQUAD:
                    max_rows(n // 16 - 1)
                for b in range(B - 1):
                    k = n - 64 * (b + 2)
                    if 0 <= k < STAGES_RUN:
                        sort_b(b, [k])
                if 0 <= n - 64 * 3 - STAGES_RUN < STAGES_PAIR - STAGES_RUN:
                    merge(1, [n - 64 * 3])

            sort_b(B - 1, range(STAGES_RUN))
            merge(B // 2, range(STAGES_RUN, STAGES_PAIR))
            for k in range(STAGES_PAIR, len(SORT)):
                sort_stage(k, 0, HALF)
            V.engine_nop().then_inc(swap_in, 1)
            dve.wait_ge(swapped, 32)
            V.tensor_tensor(ping[1][0:64, :], ping[0][0:64, :], other[0:64, ::-1], ALU.max)
            link(V.tensor_tensor(ping[1][64:128, :], other[64:128, :], ping[0][64:128, ::-1], ALU.min))
            src, side = ping[1], 0
            k = HALF // 2
            while k >= GRP:
                dst = ping[side]
                s_, d_ = (t[:, :].rearrange("p (n a k) -> p n a k", a=2, k=k) for t in (src, dst))
                exchange(d_[:, :, 0], d_[:, :, 1], s_[:, :, 0], s_[:, :, 1])
                src, side = dst, 1 - side
                k //= 2
            blocks = src[:, :].rearrange("p (n k) -> p n k", k=GRP)
            V.tensor_reduce(gsum[:, :], blocks, AX, ALU.add)
            V.tensor_reduce(gmin[:, :], blocks, AX, ALU.min)

            link(V.memset(prefix[:, :], 0))
            dve.wait_ge(loaded_ffn, 112)
            asks = [0]

            def ask():
                asks[0] += 1
                V.engine_nop().then_inc(rmat_in, 1)
                dve.wait_ge(rmat_out, asks[0])

            for s in range(DIGITS):
                link(V.tensor_tensor(cand[:, :], kdig_s[:, s], prefix[:, :].broadcast_to([P, 16]), ALU.bitwise_or))
                link(V.tensor_tensor(ge[:, :, :], gsum[:, :].unsqueeze(1).broadcast_to([P, 16, NB]),
                                     cand[:, :].bitcast(F32).unsqueeze(2).broadcast_to([P, 16, NB]), ALU.is_ge))
                link(V.tensor_reduce(cnt[:, :], ge[:, :, :], AX, ALU.add))
                ask()
                link(V.scalar_tensor_tensor(out=pick[:, :], in0=misc[:, 0:16], scalar=float(BUDGET),
                                            in1=cand[:, :].bitcast(F32), op0=ALU.is_ge, op1=ALU.mult))
                link(V.tensor_reduce(prefix[:, :].bitcast(F32), pick[:, :], AX, ALU.max))
            least = prefix[:, :].bitcast(F32)
            V.tensor_scalar(gt[:, :], gsum[:, :], least, None, ALU.is_gt, ALU.add, accum_out=one[:, 0:1])
            link(V.tensor_scalar(eq[:, :], gsum[:, :], least, None, ALU.is_equal, ALU.add, accum_out=one[:, 1:2]))
            ask()
            link(V.tensor_copy(rt[:, 0:34], misc[:, 0:34]))
            V.tensor_scalar(one[:, 2:3], rt[:, 0:1], -1.0, float(BUDGET), ALU.mult, ALU.add)
            link(V.tensor_tensor_scan(gr[:, 0], rt[:, 17:33], rt[:, 17:33], 0.0, ALU.add, ALU.max))
            link(V.scalar_tensor_tensor(out=gr[:, 1], in0=gr[:, 0], scalar=rt[:, 33:34], in1=rt[:, 1:17],
                                        op0=ALU.add, op1=ALU.add))
            link(V.tensor_tensor(gr[:, 2], gr[:, 1], rt[:, 17:33], ALU.subtract))
            link(V.scalar_tensor_tensor(out=gr[:, 3], in0=gr[:, 2], scalar=one[:, 2:3], in1=eq[:, :],
                                        op0=ALU.is_lt, op1=ALU.mult))
            link(V.tensor_tensor(gr[:, 4], gr[:, 3], gt[:, :], ALU.add))
            V.tensor_reduce(one[:, 7:8], gr[:, 4], AX, ALU.add)
            link(V.tensor_scalar(gr[:, 5], gr[:, 4], -3.0, 3.0, ALU.mult, ALU.add))
            link(V.tensor_tensor(gr[:, 0], gr[:, 5], gmin[:, :], ALU.max))
            link(V.tensor_reduce(one[:, 4:5], gr[:, 0], AX, ALU.min))
            ask()
            link(V.tensor_copy(trow[:, 0:P], misc[0:1, 0:P]))
            for k in range(2):
                last = V.tensor_tensor(trow[:, P + E * k:P + E * k + E], trow[:, 0:E], trow[:, E:P], ALU.min)
            link(last)
            ask()
            link(V.tensor_copy(one[:, 5:6], misc[:, P:P + 1]))
            V.tensor_scalar(ping[0][:, :], scT[:, :], one[:, 5:6], None, ALU.is_gt, ALU.add, accum_out=one[:, 6:7])
            for b in range(B):
                c = RUN * b
                last = V.tensor_scalar(ping[1][:, c:c + RUN], scT[:, c:c + RUN], one[:, 5:6], None, ALU.is_equal,
                                       ALU.add, accum_out=eqc[:, b:b + 1])
            link(last)
            V.engine_nop().then_inc(rmat_in, 1)
            asks[0] += 1
            V.scalar_tensor_tensor(out=ping[0][:, :], in0=scT[:, :], scalar=one[:, 5:6], in1=scT[:, :],
                                   op0=ALU.is_gt, op1=ALU.mult)
            V.tensor_scalar(scT[:, :], scT[:, :], one[:, 5:6], one[:, 5:6], ALU.is_equal, ALU.mult)
            link(V.tensor_tensor_scan(eqo[:, 2], eqc[:, :], eqc[:, :], 0.0, ALU.add, ALU.max))
            link(V.tensor_tensor(eqo[:, 3], eqo[:, 2], eqc[:, :], ALU.subtract))
            dve.wait_ge(rmat_out, asks[0])
            link(V.tensor_copy(rt[:, 0:2 + 2 * B], misc[:, 0:2 + 2 * B]))
            link(V.scalar_tensor_tensor(out=one[:, 9:10], in0=rt[:, 1:2], scalar=float(GRP), in1=rt[:, 0:1],
                                        op0=ALU.mult, op1=ALU.subtract))
            link(V.tensor_tensor_scan(eqo[:, 0], rt[:, 2:2 + B], rt[:, 2:2 + B], 0.0, ALU.add, ALU.max))
            link(V.tensor_tensor(eqo[:, 1], eqo[:, 0], rt[:, 2 + B:2 + 2 * B], ALU.subtract))
            link(V.tensor_tensor(eqo[:, 1], eqo[:, 1], eqo[:, 3], ALU.add))
            for b in range(B):
                c = RUN * b
                last = V.tensor_tensor_scan(other[:, c:c + RUN], ping[1][:, c:c + RUN], ping[1][:, c:c + RUN],
                                            eqo[:, 1, b:b + 1], ALU.add, ALU.max)
            link(last)
            link(V.scalar_tensor_tensor(out=other[:, :], in0=other[:, :], scalar=one[:, 9:10], in1=scT[:, :],
                                        op0=ALU.is_le, op1=ALU.mult))
            link(V.tensor_tensor(ping[0][:, :], ping[0][:, :], other[:, :], ALU.add))
            link(V.tensor_copy(fsp[:, 0], ping[0][:, :]))
            V.engine_nop().then_inc(fsp_ready, 1)
            link(V.tensor_tensor(ping[1][:, :], ping[0][:, :], fsp[:, 0], ALU.subtract))
            link(V.tensor_copy(fsp[:, 1], ping[1][:, :]))
            V.engine_nop().then_inc(fsp_ready, 1)
            V.tensor_tensor(fsp[:, 2], ping[1][:, :], fsp[:, 1], ALU.subtract).then_inc(fsp_ready, 1)
            dve.wait_ge(den_done, 1)
            link(V.tensor_scalar(rtok[:, :], misc[:, 0:NT * B], 1e-6, None, ALU.add))
            link(V.reciprocal(rtok[:, :], rtok[:, :]))

            def finish(blk):
                dve.wait_ge(yt_filled, blk + 1)
                if blk >= 2:
                    dve.wait_ge(stored[blk % 2], 16 * (blk // 2))
                for i in range(NT):
                    k = NT * blk + i
                    last = V.scalar_tensor_tensor(out=y_s[:, blk % 2, i], in0=misc[:, P * i:P * i + P],
                                                  scalar=rtok[:, k:k + 1], in1=x2[:, blk, i],
                                                  op0=ALU.mult, op1=ALU.add)
                last.then_inc(y_ready, 1)

            for t in range(B * NE):
                blk, n = divmod(t, NE)
                if t < EARLY:
                    u = early_u[t]
                    dve.wait_ge(early_done, t + 1)
                else:
                    u = u_s[:, t % 2]
                    dve.wait_ge(gate_filled, t + 1)
                    dve.wait_ge(silu_done, t + 1)
                    if t >= 2:
                        dve.wait_ge(h_done, t - 1)
                    V.scalar_tensor_tensor(out=u, in0=stp[:, 0, t % 2], scalar=cols_s[:, CGT + n:CGT + n + 1],
                                           in1=act_s[:, t % 2], op0=ALU.add, op1=ALU.mult).then_inc(u_done, 1)
                    dve.wait_ge(u_done, t + 1 - EARLY)
                dve.wait_ge(mask_filled, t + 1)
                if t >= 3:
                    dve.wait_ge(down_done, t - 2)
                if t < DIRECT:
                    for half in range(2):
                        c = RUN * half
                        last = V.tensor_tensor(h_s[:, t % 3, c:c + RUN], stp[:, 1 - half, t % 2, 0:RUN],
                                               u[:, c:c + RUN], ALU.mult)
                    last.then_inc(h_done, 1)
                else:
                    V.tensor_tensor(h_s[:, t % 3], stp[:, 1, t % 2], u, ALU.mult).then_inc(h_done, 1)
                if n == 6 and blk:
                    finish(blk - 1)
            finish(B - 1)
    return nc


def kernel(**inputs):
    import numpy as np
    import concourse.bacc as bacc
    from concourse.bass_utils import run_bass_kernel_spmd as run

    f = {k: np.asarray(v) for k, v in inputs.items()}
    a = {k[8:]: v for k, v in f.items() if k.startswith("L0_attn_")}
    m = {k[7:]: v for k, v in f.items() if k.startswith("L0_ffn_")}
    order = np.arange(D).reshape(2, 8, HD).transpose(0, 2, 1).reshape(-1)
    swap = order ^ 1
    worder = np.arange(D).reshape(2, 2, 2, 2, HD).transpose(1, 0, 2, 3, 4).reshape(-1)
    wa = np.concatenate([a["Wd_q_w"], a["Wd_kv_w"], a["Wk_r_w"][:, order], a["Wk_r_w"][:, swap],
                         m["Wr"], a["Wo_w"][worder]], axis=1)
    wb = np.concatenate([np.concatenate([a["Wu_q_w"][:, order], a["Wq_r_w"][:, order], a["Wq_r_w"][:, swap]], axis=1),
                         np.concatenate([a["Wu_k_w"][:, order], a["Wu_v_w"], np.zeros((LAT, D), np.float32)], axis=1)])
    cols = np.concatenate([np.concatenate([a["Wd_q_b"], a["Wd_kv_b"]])[:, None],
                           a["Wu_q_b"][order][:, None], a["Wq_r_b"][order][:, None], a["Wq_r_b"][swap][:, None],
                           a["Wu_k_b"][order][:, None], a["Wk_r_b"][order][:, None], a["Wk_r_b"][swap][:, None],
                           m["bup"].reshape(NE, P).T, m["bgate"].reshape(NE, P).T], axis=1)
    rows = np.concatenate([a["Wu_v_b"], a["Wo_b"], m["br"]])[None]
    wup = m["Wup"].transpose(1, 0, 2).reshape(D, E * HE)
    wgate = m["Wgate"].transpose(1, 0, 2).reshape(D, E * HE)
    wdown = m["Wdown"].reshape(NE, P, D).transpose(1, 0, 2).reshape(P, NE * D)

    one = np.float32(1)
    ids = np.arange(D // 2, dtype=np.float32)
    theta = np.power(np.float32(10000.0), np.float32(-2.0) * ids) / np.float32(D // 2)
    angle = np.arange(S, dtype=np.float32)[:, None] * theta[None, :]
    cos, sin = np.cos(angle).T, np.sin(angle).T
    sign = np.where(order % 2 == 0, -one, one)[:, None]
    p = np.arange(P)
    half, ex = p // E, p % E
    same = half[:, None] == half[None, :]
    trig = np.concatenate([np.eye(P, dtype=np.float32), cos[order // 2], sin[order // 2] * sign], axis=1)
    cst = np.concatenate([
        (same & (ex[:, None] < ex[None, :])), same, (half[:, None] < half[None, :]),
        (ex[:, None] == ex[None, :]), (ex[:, None] == ex[None, :]) & ~same,
        (ex[:, None] == ex[None, :]) & (half[:, None] > half[None, :]),
        np.ones((P, P))], axis=1).astype(np.float32)
    selc = np.zeros((3, 32, 8, EPT, HE), np.float32)
    for n in range(8):
        for e in range(EPT):
            selc[:, EPT * n + e, n, e, :] = 1
    selc = selc.reshape(96, 8 * P)
    kdig = np.array([[k << (4 * (DIGITS - 1 - s)) for k in range(8 if s == 0 else 16)] + [0] * (8 if s == 0 else 0)
                     for s in range(DIGITS)], np.int32)
    kdig = np.broadcast_to(kdig.reshape(1, -1), (P, DIGITS * 16))

    arrays = dict(x=f["L0_attn_x"], wa=wa, wb=wb, cols=cols, rows=rows, wup=wup, wgate=wgate, wdown=wdown,
                  bdown=m["bdown"], trig=trig, cst=cst, selc=selc, kdig=kdig)
    arrays = {k: np.ascontiguousarray(v) for k, v in arrays.items()}
    nc = bacc.Bacc("TRN2", target_bir_lowering=False, num_devices=1)
    args = [nc.dram_tensor(k, v.shape, mybir.dt.from_np(v.dtype), kind="ExternalInput").ap() for k, v in arrays.items()]
    out = nc.dram_tensor("out", (B, S, D), F32, kind="ExternalOutput").ap()
    build(nc, *args, out)
    r = run(nc, [arrays], core_ids=[0])
    return r.results[0]["out"]
```
